# Optimizing a Trainium2 kernel written in Bass

```python
import numpy as np
import jax
import jax.numpy as jnp

def _softmax(x, axis=-1):
    return jax.nn.softmax(x, axis=axis)

def _gelu(x):
    return jax.nn.gelu(x, approximate=True)

def _silu(x):
    return jax.nn.silu(x)

def _sigmoid(x):
    return jax.nn.sigmoid(x)

def _layernorm(x, axis=-1, eps=1e-05):
    m = jnp.mean(x, axis=axis, keepdims=True)
    v = jnp.var(x, axis=axis, keepdims=True)
    return (x - m) / jnp.sqrt(v + eps)

def _scatter_add(tgt, idx, src, axis=0):
    return tgt.at[idx].add(src)

def _segment_sum(src, seg, n):
    return jax.ops.segment_sum(src, seg, n)
kernel_name = 'mk_gnn_ffn_d2_gnn_r8_391807'

def setup_inputs(seed: int=0):
    np.random.seed(seed)
    _w = jnp.asarray

    def _rec_inputs():
        import jax
        import jax.numpy as jnp
        _gk = jax.random.key(seed)
        x = -0.0002928 + 1 * jax.random.normal(jax.random.fold_in(_gk, 1), (1024, 512), jnp.float32)
        _s = jax.random.randint(jax.random.fold_in(_gk, 2), (8192,), 0, 1024, jnp.int32)
        _d = jax.random.randint(jax.random.fold_in(_gk, 3), (8192,), 0, 1024, jnp.int32)
        _loop = jnp.arange(1024, dtype=jnp.int32)
        src = jnp.concatenate([_s, _d, _loop])
        dst = jnp.concatenate([_d, _s, _loop])
        _o = jnp.argsort(dst, stable=True)
        src = src[_o]
        dst = dst[_o]
        return (x, src, dst)
    x, src, dst = _rec_inputs()

    def _L0_gnn_setup():
        import jax, jax.numpy as jnp
        import numpy as np
        N = 1024
        D = 512
        E = 32768
        STEPS = 3
        key = jax.random.key(seed)
        k1, k2, k3 = jax.random.split(key, 3)
        x = jax.random.normal(k1, (N, D), dtype=jnp.float32)
        edge_index = jax.random.randint(k2, (2, E), 0, N, dtype=jnp.int32)
        W = jax.random.normal(k3, (D, D), dtype=jnp.float32) / np.sqrt(D)
        b = jnp.zeros((D,), dtype=jnp.float32)
        diffusion_weights = jnp.ones((STEPS + 1,), dtype=jnp.float32) / (STEPS + 1)
        return {'x': x, 'edge_index': edge_index, 'W': W, 'b': b, 'diffusion_weights': diffusion_weights}
    _L0_gnn_all = _L0_gnn_setup()
    _L0_gnn_in = {k: v for k, v in _L0_gnn_all.items() if k in ('W', 'b', 'diffusion_weights')}
    del _L0_gnn_all

    def _L0_ffn_setup():
        import jax, jax.numpy as jnp
        import numpy as np
        B, S, D, H, E, K = (2, 1024, 512, 256, 64, 2)
        EPS = 1e-05
        key = jax.random.key(seed)
        ks = jax.random.split(key, 5)
        s = 0.02
        return {'x': jax.random.normal(ks[0], (B, S, D), dtype=jnp.float32), 'Wg': jax.random.normal(ks[1], (D, E), dtype=jnp.float32) * s, 'bg': jnp.zeros((E,), dtype=jnp.float32), 'W1': jax.random.normal(ks[2], (E, D, H), dtype=jnp.float32) * s, 'b1': jnp.zeros((E, H), dtype=jnp.float32), 'W2': jax.random.normal(ks[3], (E, H, D), dtype=jnp.float32) * s, 'b2': jnp.zeros((E, D), dtype=jnp.float32), 'gamma': jnp.ones((D,), dtype=jnp.float32), 'beta': jnp.zeros((D,), dtype=jnp.float32)}
    _L0_ffn_all = _L0_ffn_setup()
    _L0_ffn_in = {k: v for k, v in _L0_ffn_all.items() if k in ('Wg', 'bg', 'W1', 'b1', 'W2', 'b2', 'gamma', 'beta')}
    del _L0_ffn_all

    def _L1_gnn_setup():
        import jax, jax.numpy as jnp
        import numpy as np
        NEG_SLOPE = 0.2
        HEADS = 8

        def gat_conv(x, src, dst, W, att_src, att_dst, bias, heads, out_ch):
            N = x.shape[0]
            h = (x @ W).reshape(N, heads, out_ch)
            a_src = jnp.einsum('nhc,hc->nh', h, att_src)
            a_dst = jnp.einsum('nhc,hc->nh', h, att_dst)
            e = jax.nn.leaky_relu(a_src[src] + a_dst[dst], NEG_SLOPE)
            m = jax.ops.segment_max(e, dst, num_segments=N)
            m = jnp.where(jnp.isfinite(m), m, jnp.zeros_like(m))
            ex = jnp.exp(e - m[dst])
            s = jax.ops.segment_sum(ex, dst, num_segments=N)
            alpha = ex / (s[dst] + 1e-16)
            msg = h[src] * alpha[:, :, None]
            out = jax.ops.segment_sum(msg, dst, num_segments=N)
            return out.reshape(N, heads * out_ch) + bias
        key = jax.random.key(seed)
        ks = jax.random.split(key, 12)
        N, F_in, nhid, heads, ncls, E = (2500, 512, 128, HEADS, 64, 25000)
        x = jax.random.normal(ks[0], (N, F_in), dtype=jnp.float32)
        edge_index = jax.random.randint(ks[1], (2, E), 0, N, dtype=jnp.int32)

        def lin(k, fi, fo):
            return jax.random.normal(k, (fi, fo), dtype=jnp.float32) / np.sqrt(fi)
        W1 = lin(ks[2], F_in, heads * nhid)
        att_src1 = jax.random.normal(ks[3], (heads, nhid), dtype=jnp.float32) / np.sqrt(nhid)
        att_dst1 = jax.random.normal(ks[4], (heads, nhid), dtype=jnp.float32) / np.sqrt(nhid)
        b1 = jnp.zeros((heads * nhid,), dtype=jnp.float32)
        W2 = lin(ks[5], heads * nhid, heads * ncls)
        att_src2 = jax.random.normal(ks[6], (heads, ncls), dtype=jnp.float32) / np.sqrt(ncls)
        att_dst2 = jax.random.normal(ks[7], (heads, ncls), dtype=jnp.float32) / np.sqrt(ncls)
        b2 = jnp.zeros((heads * ncls,), dtype=jnp.float32)
        return {'x': x, 'edge_index': edge_index, 'W1': W1, 'att_src1': att_src1, 'att_dst1': att_dst1, 'b1': b1, 'W2': W2, 'att_src2': att_src2, 'att_dst2': att_dst2, 'b2': b2}
    _L1_gnn_all = _L1_gnn_setup()
    _L1_gnn_in = {k: v for k, v in _L1_gnn_all.items() if k in ('W1', 'att_src1', 'att_dst1', 'b1', 'W2', 'att_src2', 'att_dst2', 'b2')}
    del _L1_gnn_all

    def _L1_ffn_setup():
        import jax, jax.numpy as jnp
        import numpy as np
        B, S, D = (8, 512, 512)
        H = 256
        O = 512
        E = 8
        TOP_K = 1
        key = jax.random.key(seed)
        ks = jax.random.split(key, 8)
        sc = 0.02
        return {'x': jax.random.normal(ks[0], (B, S, D), dtype=jnp.float32), 'Wr': jax.random.normal(ks[1], (D, E), dtype=jnp.float32) * sc, 'br': jnp.zeros((E,), dtype=jnp.float32), 'W1': jax.random.normal(ks[2], (E, D, H), dtype=jnp.float32) * sc, 'b1': jnp.zeros((E, H), dtype=jnp.float32), 'W2': jax.random.normal(ks[3], (E, H, O), dtype=jnp.float32) * sc, 'b2': jnp.zeros((E, O), dtype=jnp.float32)}
    _L1_ffn_all = _L1_ffn_setup()
    _L1_ffn_in = {k: v for k, v in _L1_ffn_all.items() if k in ('Wr', 'br', 'W1', 'b1', 'W2', 'b2')}
    del _L1_ffn_all
    return {'x': x, 'src': src, 'dst': dst, 'L0_gnn_W': _L0_gnn_in['W'], 'L0_gnn_b': _L0_gnn_in['b'], 'L0_gnn_diffusion_weights': _L0_gnn_in['diffusion_weights'], 'L0_ffn_Wg': _L0_ffn_in['Wg'], 'L0_ffn_bg': _L0_ffn_in['bg'], 'L0_ffn_W1': _L0_ffn_in['W1'], 'L0_ffn_b1': _L0_ffn_in['b1'], 'L0_ffn_W2': _L0_ffn_in['W2'], 'L0_ffn_b2': _L0_ffn_in['b2'], 'L0_ffn_gamma': _L0_ffn_in['gamma'], 'L0_ffn_beta': _L0_ffn_in['beta'], 'L1_gnn_W1': _L1_gnn_in['W1'], 'L1_gnn_att_src1': _L1_gnn_in['att_src1'], 'L1_gnn_att_dst1': _L1_gnn_in['att_dst1'], 'L1_gnn_b1': _L1_gnn_in['b1'], 'L1_gnn_W2': _L1_gnn_in['W2'], 'L1_gnn_att_src2': _L1_gnn_in['att_src2'], 'L1_gnn_att_dst2': _L1_gnn_in['att_dst2'], 'L1_gnn_b2': _L1_gnn_in['b2'], 'L1_ffn_Wr': _L1_ffn_in['Wr'], 'L1_ffn_br': _L1_ffn_in['br'], 'L1_ffn_W1': _L1_ffn_in['W1'], 'L1_ffn_b1': _L1_ffn_in['b1'], 'L1_ffn_W2': _L1_ffn_in['W2'], 'L1_ffn_b2': _L1_ffn_in['b2']}

def reference(x, src, dst, L0_gnn_W, L0_gnn_b, L0_gnn_diffusion_weights, L0_ffn_Wg, L0_ffn_bg, L0_ffn_W1, L0_ffn_b1, L0_ffn_W2, L0_ffn_b2, L0_ffn_gamma, L0_ffn_beta, L1_gnn_W1, L1_gnn_att_src1, L1_gnn_att_dst1, L1_gnn_b1, L1_gnn_W2, L1_gnn_att_src2, L1_gnn_att_dst2, L1_gnn_b2, L1_ffn_Wr, L1_ffn_br, L1_ffn_W1, L1_ffn_b1, L1_ffn_W2, L1_ffn_b2):
    import jax
    import jax.numpy as jnp

    def _L0_gnn_ref(x, edge_index, W, b, diffusion_weights):
        import jax, jax.numpy as jnp
        import numpy as np
        N = 1024
        D = 512
        E = 32768
        STEPS = 3
        h = x @ W + b
        row, col = (edge_index[0], edge_index[1])
        adj = jnp.zeros((N, N), dtype=h.dtype)
        adj = adj.at[row, col].set(1.0)
        adj = adj.at[col, row].set(1.0)
        adj = adj + jnp.eye(N, dtype=h.dtype)
        row_sum = adj.sum(axis=1, keepdims=True)
        adj = adj / jnp.maximum(row_sum, 1.0)
        out = diffusion_weights[0] * h
        cur = h
        for i in range(STEPS):
            cur = adj @ cur
            out = out + diffusion_weights[i + 1] * cur
        return jax.nn.relu(out)

    def _L0_ffn_ref(x, Wg, bg, W1, b1, W2, b2, gamma, beta):
        import jax, jax.numpy as jnp
        import numpy as np
        B, S, D, H, E, K = (2, 1024, 512, 256, 64, 2)
        EPS = 1e-05
        probs = jax.nn.softmax(x @ Wg + bg, axis=-1)
        topk_vals, topk_idx = jax.lax.top_k(probs, K)
        sparse_w = jnp.sum(jax.nn.one_hot(topk_idx, E, dtype=probs.dtype) * topk_vals[..., None], axis=-2)
        h = jax.nn.relu(jnp.einsum('bsd,edh->bseh', x, W1) + b1)
        expert_out = jnp.einsum('bseh,ehd->bsed', h, W2) + b2
        out = jnp.einsum('bse,bsed->bsd', sparse_w, expert_out) + x
        mu = out.mean(-1, keepdims=True)
        var = ((out - mu) ** 2).mean(-1, keepdims=True)
        return (out - mu) * jax.lax.rsqrt(var + EPS) * gamma + beta

    def _L1_gnn_ref(x, edge_index, W1, att_src1, att_dst1, b1, W2, att_src2, att_dst2, b2):
        import jax, jax.numpy as jnp
        import numpy as np
        NEG_SLOPE = 0.2
        HEADS = 8

        def gat_conv(x, src, dst, W, att_src, att_dst, bias, heads, out_ch):
            N = x.shape[0]
            h = (x @ W).reshape(N, heads, out_ch)
            a_src = jnp.einsum('nhc,hc->nh', h, att_src)
            a_dst = jnp.einsum('nhc,hc->nh', h, att_dst)
            e = jax.nn.leaky_relu(a_src[src] + a_dst[dst], NEG_SLOPE)
            m = jax.ops.segment_max(e, dst, num_segments=N)
            m = jnp.where(jnp.isfinite(m), m, jnp.zeros_like(m))
            ex = jnp.exp(e - m[dst])
            s = jax.ops.segment_sum(ex, dst, num_segments=N)
            alpha = ex / (s[dst] + 1e-16)
            msg = h[src] * alpha[:, :, None]
            out = jax.ops.segment_sum(msg, dst, num_segments=N)
            return out.reshape(N, heads * out_ch) + bias
        N = x.shape[0]
        nhid = att_src1.shape[1]
        ncls = att_src2.shape[1]
        loop = jnp.arange(N, dtype=edge_index.dtype)
        src = jnp.concatenate([edge_index[0], loop])
        dst = jnp.concatenate([edge_index[1], loop])
        h = gat_conv(x, src, dst, W1, att_src1, att_dst1, b1, HEADS, nhid)
        h = jax.nn.relu(h)
        out = gat_conv(h, src, dst, W2, att_src2, att_dst2, b2, HEADS, ncls)
        return jax.nn.log_softmax(out, axis=1)

    def _L1_ffn_ref(x, Wr, br, W1, b1, W2, b2):
        import jax, jax.numpy as jnp
        import numpy as np
        B, S, D = (8, 512, 512)
        H = 256
        O = 512
        E = 8
        TOP_K = 1
        b, s, d = x.shape
        xf = x.reshape(-1, d)
        router_logits = xf @ Wr + br
        topk_logits, topk_idx = jax.lax.top_k(router_logits, TOP_K)
        topk_gates = jax.nn.softmax(topk_logits, axis=1)
        out = jnp.zeros((xf.shape[0], O), dtype=x.dtype)
        for k in range(TOP_K):
            idx_k = topk_idx[:, k]
            gate_k = topk_gates[:, k:k + 1]
            for e in range(E):
                h = jax.nn.relu(xf @ W1[e] + b1[e])
                oe = h @ W2[e] + b2[e]
                mask = (idx_k == e)[:, None]
                out = out + jnp.where(mask, gate_k * oe, 0.0)
        return out.reshape(b, s, O)
    edge_index = jnp.stack([src, dst])
    x = x + _L0_gnn_ref(_layernorm(x, axis=-1), edge_index, L0_gnn_W, L0_gnn_b, L0_gnn_diffusion_weights)
    x = x + _L0_ffn_ref(_layernorm(x, axis=-1)[None], L0_ffn_Wg, L0_ffn_bg, L0_ffn_W1, L0_ffn_b1, L0_ffn_W2, L0_ffn_b2, L0_ffn_gamma, L0_ffn_beta)[0]
    x = x + _L1_gnn_ref(_layernorm(x, axis=-1), edge_index, L1_gnn_W1, L1_gnn_att_src1, L1_gnn_att_dst1, L1_gnn_b1, L1_gnn_W2, L1_gnn_att_src2, L1_gnn_att_dst2, L1_gnn_b2)
    x = x + _L1_ffn_ref(_layernorm(x, axis=-1)[None], L1_ffn_Wr, L1_ffn_br, L1_ffn_W1, L1_ffn_b1, L1_ffn_W2, L1_ffn_b2)[0]
    return x

_drawn_inputs = setup_inputs


def setup_inputs(seed=0):
    import zlib

    import numpy as np

    out = dict(_drawn_inputs(seed))
    spreads = {'L0_gnn_b': (0.0, 0.376),
     'L0_gnn_diffusion_weights': (0.25, 0.6),
     'L0_ffn_bg': (0.0, 0.8),
     'L0_ffn_b1': (0.0, 0.8),
     'L0_ffn_b2': (0.0, 0.8),
     'L0_ffn_gamma': (1.0, 0.2),
     'L0_ffn_beta': (0.0, 0.498),
     'L1_gnn_b1': (0.0, 0.8),
     'L1_gnn_b2': (0.0, 0.454),
     'L1_ffn_br': (0.0, 0.711),
     'L1_ffn_b1': (0.0, 0.8),
     'L1_ffn_b2': (0.0, 0.518)}
    factors = {'L0_ffn_Wg': 8.0,
     'L0_ffn_W1': 8.0,
     'L0_ffn_W2': 8.0,
     'L1_gnn_W1': 4.125,
     'L1_gnn_att_src1': 5.874,
     'L1_gnn_att_dst1': 8.0,
     'L1_gnn_att_src2': 8.0,
     'L1_gnn_att_dst2': 8.0,
     'L1_ffn_Wr': 2.69,
     'L1_ffn_W1': 4.273,
     'L1_ffn_W2': 3.468}
    for name, (base, spread) in spreads.items():
        noise = np.random.default_rng([zlib.crc32(name.encode()), seed]).standard_normal(out[name].shape)
        drawn = base * np.exp(spread * noise) if base else spread * noise
        out[name] = jnp.asarray(drawn.astype(out[name].dtype))
    for name, factor in factors.items():
        out[name] = (out[name] * factor).astype(out[name].dtype)
    return out
```

```python
from contextlib import ExitStack

import concourse.bass as bass
from concourse import mybir

ALU = mybir.AluOpType
ACT = mybir.ActivationFunctionType
F32 = mybir.dt.float32
F32R = mybir.dt.float32r
BF16 = mybir.dt.bfloat16
F16 = mybir.dt.float16
I32 = mybir.dt.int32
U32 = mybir.dt.uint32
X = mybir.AxisListType.X
RMAX = bass.bass_isa.ReduceOp.max

P = 128
KIB = 1024
NEG = -1.0e30
LN_EPS = 1e-5
NEG_SLOPE = 0.2
NO_ROW = 1 << 20


def build(nc, ins, out):
    x_d, src_d, dst_d = ins["x"], ins["src"], ins["dst"]
    N, D = x_d.shape
    E = src_d.shape[0]
    NT = N // P
    KD = D // P
    STEPS = ins["L0_gnn_diffusion_weights"].shape[0] - 1
    NX0, H = ins["L0_ffn_W1"].shape[0], ins["L0_ffn_W1"].shape[2]
    NX1 = ins["L1_ffn_W1"].shape[0]
    HC = H // P
    TOPK = 2
    HEADS, CH1 = ins["L1_gnn_att_src1"].shape
    CH2 = ins["L1_gnn_att_src2"].shape[1]
    F1 = HEADS * CH1
    KF = F1 // P
    EP = 2 * P
    EQ = E // EP
    assert E % EP == 0 and EQ <= P and N == 8 * P

    ctx = ExitStack()
    with ctx:
        used = []

        def sem(name):
            used.append(nc.alloc_semaphore(name))
            return used[-1]

        def lasting(name):
            return nc.alloc_semaphore(name)

        def recycle():
            nc.clear_and_free_semaphores(list(used))
            nc.all_engine_barrier()
            used.clear()

        def place(name, shape, dt, at):
            return nc.alloc_sbuf_tensor_at(name, shape, dt, offset=BASE + at)

        ARENA = 207 * KIB + 512
        BASE = (nc.sbuf_base + 31) // 32 * 32
        ctx.enter_context(nc.sbuf_tensor("arena", [P, ARENA // 4], F32))
        PS = ctx.enter_context(nc.psum_tensor("PS", [P, 8, 512], F32))

        x = place("x_res", [P, NT, D], F32, 0)
        xln = place("xln", [P, NT, D], F32, 16 * KIB)
        xT = place("xT", [P, KD, N], F32, 32 * KIB)
        CT = place("CT", [P, NT, N], F32, 48 * KIB)
        mask = place("mask", [P, NT, N], BF16, 80 * KIB)
        iota = place("iota", [P, N], F16, 96 * KIB)
        ident = place("ident", [P, P], F32, 98 * KIB)
        onesb = place("onesb", [P, P], BF16, 98 * KIB + 512)
        before = place("before", [P, P], BF16, 98 * KIB + 768)
        zerob = place("zerob", [P, 512], BF16, 99 * KIB)
        iotaf = place("iotaf", [P, NX0], F32, 100 * KIB)
        ones1 = place("ones1", [1, P], F32, 100 * KIB + 256)
        tokid = place("tokid", [P, NT, TOPK], I32, 100 * KIB + 768)
        st = place("st", [P, NT, 6], F32, 101 * KIB)
        mv = place("mv", [P, NT, 2], F32, 101 * KIB + 256)
        ve = place("ve", [P, NT], F32, 101 * KIB + 320)
        sq = place("sq", [P, NT], F32, 101 * KIB + 352)
        rs = place("rs", [P, NT], F32, 101 * KIB + 384)
        tq = place("tq", [P, NT], F32, 101 * KIB + 416)
        rowsum = place("rowsum", [P, NT], F32, 101 * KIB + 448)
        rinv = place("rinv", [P, NT], F32, 101 * KIB + 480)
        wdiff = place("wdiff", [P, STEPS + 1], F32, 101 * KIB + 512)
        nmt = place("nmt", [P, NT], F32, 101 * KIB + 544)

        xrow_dram = nc.dram_tensor("xrow_scratch", (N, D), F32, kind="Internal").ap()
        y_dram = nc.dram_tensor("y_scratch", (N * TOPK, D), F32, kind="Internal").ap()
        z_dram = nc.dram_tensor("z_scratch", (N, D), F32, kind="Internal").ap()
        NB0 = NX0 + (N * TOPK) // (P + 1)
        NB1 = NX1 + (N - NX1) // P
        slot0_dram = nc.dram_tensor("slot0_scratch", (P * NB0, 1), I32, kind="Internal").ap()
        slot1_dram = nc.dram_tensor("slot1_scratch", (P * NB1, 1), I32, kind="Internal").ap()
        a_dram = [nc.dram_tensor(f"a{n}_scratch", (2 * HEADS, N), F32, kind="Internal").ap() for n in (1, 2)]

        def bcast(v, n):
            return v.rearrange("(o n) -> o n", o=1).to_broadcast([P, n])

        def within(value, least, most):
            return nc.s_assert_within(value, least, most,
                                      skip_runtime_bounds_check_because="it follows from the loop's bounds")

        def phase():
            if len(used) > 70:
                recycle()

        def layernorm(name, src, xln, xT, keep, loaded=None):
            s_stat, s_sqrt, s_tiles = sem(name + "_stat"), sem(name + "_sqrt"), sem(name + "_tiles")
            s_turned, s_moved, s_kept = sem(name + "_turned"), sem(name + "_moved"), sem(name + "_kept")
            s_chain = sem(name + "_chain")
            with nc.Block() as block:
                @block.vector
                def _(dve):
                    n = [0]

                    def link(ins):
                        n[0] += 1
                        ins.then_inc(s_chain, 1)
                        dve.wait_ge(s_chain, n[0])

                    if loaded is not None:
                        dve.wait_ge(loaded, 16)
                    for t in range(NT):
                        last = dve.bn_stats(st[:, t, :], src[:, t, :])
                    link(last)
                    for t in range(NT):
                        last = dve.bn_aggr(mv[:, t, :], st[:, t, :])
                    link(last)
                    dve.tensor_scalar(ve[:], mv[:, :, 1], LN_EPS, None, ALU.add).then_inc(s_stat, 1)
                    dve.wait_ge(s_sqrt, 1)
                    link(dve.reciprocal(tq[:], sq[:]))
                    link(dve.tensor_tensor(tq[:], tq[:], ve[:], ALU.mult))
                    link(dve.tensor_tensor(tq[:], tq[:], sq[:], ALU.add))
                    link(dve.tensor_scalar(tq[:], tq[:], 0.5, None, ALU.mult))
                    link(dve.reciprocal(rs[:], tq[:]))
                    for t in range(NT):
                        dve.tensor_scalar(xln[:, t, :], src[:, t, :], mv[:, t, 0:1], rs[:, t:t + 1],
                                          ALU.subtract, ALU.mult).then_inc(s_tiles, 1)

                @block.scalar
                def _(act):
                    act.wait_ge(s_stat, 1)
                    act.activation(sq[:], ve[:], ACT.Sqrt).then_inc(s_sqrt, 1)
                    for t in range(NT):
                        act.wait_ge(s_turned, t + 1)
                        act.copy(xT[:, :, t * P:(t + 1) * P],
                                 PS[:, t % 2, :].rearrange("p (k n) -> p k n", k=KD)).then_inc(s_moved, 1)

                @block.tensor
                def _(pe):
                    for t in range(NT):
                        pe.wait_ge(s_tiles, t + 1)
                        if t >= 2:
                            pe.wait_ge(s_moved, t - 1)
                        for k in range(KD):
                            last = pe.transpose(PS[:, t % 2, k * P:(k + 1) * P], xln[:, t, k * P:(k + 1) * P],
                                                ident[:])
                        last.then_inc(s_turned, 1)

                if keep:
                    @block.sync
                    def _(sp):
                        sp.wait_ge(s_tiles, NT)
                        sp.dma_start(xrow_dram.rearrange("(t p) d -> p t d", p=P), xln[:]).then_inc(s_kept, 16)
                        sp.wait_ge(s_kept, 16)

        srcq = place("srcq", [EQ, EP], I32, 112 * KIB)
        dstq = place("dstq", [EQ, EP], I32, 113 * KIB)
        srcf = place("srcf", [EQ, EP], F32, 114 * KIB)
        dstf = place("dstf", [EQ, EP], F32, 115 * KIB)
        tili = place("tili", [EQ, EP], I32, 116 * KIB)
        tilf = place("tilf", [EQ, EP], F32, 117 * KIB)
        C = place("C", [P, NT, N], F32, 112 * KIB)
        adj = place("adj", [P, NT, N], F32R, 144 * KIB)
        oh_src = place("oh_src", [P, 2, 2, N], BF16, 176 * KIB)
        oh_dst = place("oh_dst", [P, 2, 2, P], BF16, 184 * KIB)
        eT = place("eT", [P, 2, 2, EQ], F32, 185 * KIB)
        W0 = place("W0", [P, KD, D], F32, 192 * KIB)
        b0 = place("b0", [P, D], F32, 200 * KIB)
        reach = place("reach", [EQ, 2 * NT], F32, 188 * KIB)
        reachm = place("reachm", [EQ, 2 * NT], F32, 188 * KIB + 64)
        tmm = place("tmm", [EQ, 2], F32, 188 * KIB + 128)
        qcol = place("qcol", [EQ, 2], F32, 188 * KIB + 160)
        act8 = place("act8", [EQ, 2, NT], F32, 188 * KIB + 192)
        rows = place("rows", [1, 6, NT], F32, 188 * KIB + 256)
        rowi = place("rowi", [1, 3, NT], I32, 188 * KIB + 512)
        both = place("both", [P, 2, N], F32, 176 * KIB)

        s_in_x, s_in_e, s_in_w = lasting("in_x"), lasting("in_edges"), lasting("in_w")

        phase()
        s_const, s_eflt, s_eturn, s_eT = sem("const"), sem("edges_float"), sem("edges_turned"), sem("eT_ready")
        s_reach, s_reachm, s_range = sem("reach"), sem("reach_max"), sem("range_ready")
        s_free, s_hot, s_tile, s_C = sem("onehot_free"), sem("onehot_ready"), sem("C_summed"), sem("C_moved")
        s_ctt, s_ctm, s_both, s_adj = sem("CT_turned"), sem("CT_moved"), sem("both_ready"), sem("adj_moved")
        s_chain, s_chp = sem("prep_chain"), sem("prep_chain_pool")
        with nc.Block() as block:
            @block.sync
            def _(sp):
                sp.dma_start(dstq[:], dst_d.rearrange("(q e) -> q e", e=EP)).then_inc(s_in_e, 16)
                sp.dma_start(srcq[:], src_d.rearrange("(q e) -> q e", e=EP)).then_inc(s_in_e, 16)
                sp.dma_start(x[:], x_d.rearrange("(t p) d -> p t d", p=P)).then_inc(s_in_x, 16)
                sp.dma_start(W0[:], ins["L0_gnn_W"].rearrange("(k p) n -> p k n", p=P)).then_inc(s_in_w, 16)
                sp.dma_start(b0[:], bcast(ins["L0_gnn_b"], D)).then_inc(s_in_w, 16)
                sp.dma_start(wdiff[:], bcast(ins["L0_gnn_diffusion_weights"], STEPS + 1)).then_inc(s_in_w, 16)

            @block.gpsimd
            def _(pool):
                n = [0]

                def link(ins):
                    n[0] += 1
                    ins.then_inc(s_chp, 1)
                    pool.wait_ge(s_chp, n[0])

                pool.iota(iota[:], [[1, N]], 0, 0, allow_small_or_imprecise_dtypes=True)
                pool.iota(qcol[:, 0:1], [[0, 1]], 1, 1, allow_small_or_imprecise_dtypes=True)
                pool.iota(qcol[:, 1:2], [[0, 1]], EQ, -1, allow_small_or_imprecise_dtypes=True)
                pool.iota(iotaf[:], [[1, NX0]], 0, 0, allow_small_or_imprecise_dtypes=True)
                pool.iota(tokid[:], [[TOPK * P, NT], [1, TOPK]], 0, TOPK)
                pool.memset(onesb[:], 1.0)
                pool.memset(ones1[:], 1.0)
                pool.memset(zerob[:], 0.0)
                pool.memset(ident[:], 0.0)
                link(pool.memset(before[:], 1.0))
                pool.affine_select(before[:], before[:], [[1, P]], ALU.is_gt, 0.0, base=0, channel_multiplier=-1)
                pool.affine_select(ident[:], ident[:], [[1, P]], ALU.not_equal, 1.0, base=0,
                                   channel_multiplier=-1).then_inc(s_const, 1)
                pool.wait_ge(s_reach, 1)
                pool.partition_all_reduce(reachm[:], reach[:], EQ, RMAX).then_inc(s_reachm, 1)

            @block.vector
            def _(dve):
                n = [0]

                def link(ins):
                    n[0] += 1
                    ins.then_inc(s_chain, 1)
                    dve.wait_ge(s_chain, n[0])

                dve.wait_ge(s_in_e, 32)
                dve.tensor_copy(srcf[:], srcq[:])
                dve.tensor_copy(dstf[:], dstq[:]).then_inc(s_eflt, 1)
                link(dve.tensor_scalar(tili[:], dstq[:], P.bit_length() - 1, None, ALU.logical_shift_right))
                link(dve.tensor_copy(tilf[:], tili[:]))
                dve.tensor_reduce(tmm[:, 0:1], tilf[:], X, ALU.min)
                link(dve.tensor_reduce(tmm[:, 1:2], tilf[:], X, ALU.max))
                dve.wait_ge(s_const, 1)
                dve.tensor_scalar(act8[:, 0, :], iotaf[0:EQ, 0:NT], tmm[:, 0:1], None, ALU.is_ge)
                link(dve.tensor_scalar(act8[:, 1, :], iotaf[0:EQ, 0:NT], tmm[:, 1:2], None, ALU.is_le))
                link(dve.tensor_tensor(act8[:, 0, :], act8[:, 0, :], act8[:, 1, :], ALU.mult))
                dve.tensor_scalar(reach[:, 0:NT], act8[:, 0, :], qcol[:, 0:1], None, ALU.mult)
                dve.tensor_scalar(reach[:, NT:2 * NT], act8[:, 0, :], qcol[:, 1:2], None,
                                  ALU.mult).then_inc(s_reach, 1)
                dve.wait_ge(s_eturn, 1)
                dve.tensor_copy(eT[:].rearrange("p a c q -> p (a c) q"),
                                PS[:, 0, 0:4 * EQ].rearrange("p (a q) -> p a q", a=4)).then_inc(s_eT, 1)
                dve.wait_ge(s_reachm, 1)
                LO, HI, CNT, END, BEG, DEL = (rows[:, k, :] for k in range(6))
                link(dve.tensor_scalar(LO, reachm[0:1, NT:2 * NT], -1.0, float(EQ), ALU.mult, ALU.add))
                link(dve.tensor_scalar(LO, LO, float(EQ - 1), None, ALU.min))
                link(dve.tensor_scalar(HI, LO, 1.0, None, ALU.add))
                link(dve.tensor_tensor(HI, HI, reachm[0:1, 0:NT], ALU.max))
                link(dve.tensor_tensor(CNT, HI, LO, ALU.subtract))
                link(dve.tensor_tensor_scan(END, CNT, CNT, 0.0, ALU.add, ALU.bypass))
                link(dve.tensor_tensor(BEG, END, CNT, ALU.subtract))
                link(dve.tensor_tensor(DEL, LO, BEG, ALU.subtract))
                dve.tensor_copy(rowi[:, 0, :], BEG)
                dve.tensor_copy(rowi[:, 1, :], END)
                dve.tensor_copy(rowi[:, 2, :], DEL).then_inc(s_range, 1)
                dve.wait_ge(s_range, 1)
                for t in range(NT):
                    first = dve.value_load(rowi[0:1, 0, t:t + 1], min_val=0, max_val=NT * EQ)
                    last = dve.value_load(rowi[0:1, 1, t:t + 1], min_val=1, max_val=NT * EQ)
                    shift = dve.value_load(rowi[0:1, 2, t:t + 1], min_val=-NT * EQ, max_val=EQ)
                    with dve.Fori(first, last) as u:
                        q = within(dve.snap(u + shift), 0, EQ - 1)
                        slot = within(dve.snap(u % 2), 0, 1)
                        dve.wait_ge(s_free, u + 1)
                        for c in range(2):
                            dve.tensor_scalar(oh_src[:, bass.ds(slot, 1), c, :], iota[:],
                                              eT[:, 0, c, bass.ds(q, 1)], None, ALU.is_equal)
                            ins_ = dve.tensor_scalar(oh_dst[:, bass.ds(slot, 1), c, :],
                                                     iota[:, t * P:(t + 1) * P],
                                                     eT[:, 1, c, bass.ds(q, 1)], None, ALU.is_equal)
                        ins_.then_inc(s_hot, 1)
                for i in range(NT):
                    own = slice(i * P, (i + 1) * P)
                    dve.wait_ge(s_ctt, i + 1)
                    if i >= 2:
                        dve.wait_ge(s_adj, i - 1)
                    if i == 0:
                        dve.wait_ge(s_C, NT)
                    link(dve.tensor_tensor(both[:, i % 2, :], C[:, i, :],
                                           PS[:, 4 + 2 * (i % 2):6 + 2 * (i % 2), :].rearrange("p a n -> p (a n)"),
                                           ALU.add))
                    link(dve.tensor_scalar(both[:, i % 2, :], both[:, i % 2, :], 1.0, None, ALU.min, ALU.add,
                                           accum_out=rowsum[:, i:i + 1]))
                    dve.tensor_tensor(both[:, i % 2, own], both[:, i % 2, own], ident[:],
                                      ALU.add).then_inc(s_both, 1)
                    link(dve.tensor_tensor(C[:, i, own], C[:, i, own], ident[:], ALU.add))
                    dve.wait_ge(s_ctm, i + 1)
                    dve.tensor_tensor(CT[:, i, own], CT[:, i, own], ident[:], ALU.add)
                    dve.tensor_scalar(mask[:, i, :], C[:, i, :], 0.0, NEG, ALU.is_equal, ALU.mult)
                link(dve.tensor_scalar(rowsum[:], rowsum[:], 1.0, 1.0, ALU.add, ALU.max))
                link(dve.reciprocal(rinv[:], rowsum[:]))

            @block.scalar
            def _(act):
                for t in range(NT):
                    act.wait_ge(s_tile, t + 1)
                    act.copy(C[:, t, :], PS[:, 2 * (t % 2):2 * (t % 2) + 2, :].rearrange("p a n -> p (a n)")
                             ).then_inc(s_C, 1)
                for i in range(NT):
                    act.wait_ge(s_both, i + 1)
                    act.copy(CT[:, i, :], PS[:, 4 + 2 * (i % 2):6 + 2 * (i % 2), :].rearrange("p a n -> p (a n)")
                             ).then_inc(s_ctm, 1)
                    act.copy(adj[:, i, :], both[:, i % 2, :]).then_inc(s_adj, 1)

            @block.tensor
            def _(pe):
                pe.wait_ge(s_const, 1)
                pe.wait_ge(s_eflt, 1)
                for a, e in enumerate((srcf, dstf)):
                    for c in range(2):
                        last = pe.transpose(PS[:, 0, (2 * a + c) * EQ:(2 * a + c + 1) * EQ],
                                            e[:, c * P:(c + 1) * P], ident[0:EQ, 0:EQ])
                last.then_inc(s_eturn, 1)
                pe.wait_ge(s_eT, 1)
                pe.wait_ge(s_range, 1)
                pe.sem_inc(s_free, 2)
                for t in range(NT):
                    first = pe.value_load(rowi[0:1, 0, t:t + 1], min_val=0, max_val=NT * EQ)
                    last = pe.value_load(rowi[0:1, 1, t:t + 1], min_val=1, max_val=NT * EQ)
                    if t >= 2:
                        pe.wait_ge(s_C, t - 1)
                    for h in range(2):
                        pe.matmul(PS[:, 2 * (t % 2) + h, :], onesb[:], zerob[:], start=True, stop=False)
                    with pe.Fori(first, last) as u:
                        slot = within(pe.snap(u % 2), 0, 1)
                        pe.wait_ge(s_hot, u + 1)
                        for c in range(2):
                            for h in range(2):
                                mm = pe.matmul(PS[:, 2 * (t % 2) + h, :], oh_dst[:, bass.ds(slot, 1), c, :],
                                               oh_src[:, bass.ds(slot, 1), c, h * 512:(h + 1) * 512],
                                               start=False, stop=False)
                        mm.then_inc(s_free, 1)
                    for h in range(2):
                        mm = pe.matmul(PS[:, 2 * (t % 2) + h, :], onesb[:], zerob[:], start=False, stop=True)
                    mm.then_inc(s_tile, 1)
                pe.wait_ge(s_C, NT)
                for i in range(NT):
                    if i >= 2:
                        pe.wait_ge(s_ctm, i - 1)
                    for j in range(NT):
                        mm = pe.transpose(PS[:, 4 + 2 * (i % 2) + j // 4, (j % 4) * P:(j % 4 + 1) * P],
                                          C[:, j, i * P:(i + 1) * P], ident[:])
                    mm.then_inc(s_ctt, 1)

        phase()
        layernorm("ln0", x, xln, xT, keep=False, loaded=s_in_x)
        hi = [place("hi0", [P, NT, D], F32R, 112 * KIB), place("hi1", [P, NT, D], F32R, 16 * KIB)]
        lo = [place("lo0", [P, NT, D], F32R, 128 * KIB), place("lo1", [P, NT, D], F32R, 32 * KIB)]
        acc = place("acc", [P, NT, D], F32, 176 * KIB)
        cur = place("cur", [P, 2, D], F32, 202 * KIB)
        phase()
        s_sum, s_cur, s_hi, s_lo, s_acc = (sem("gnn_" + k) for k in ("sum", "cur", "hi", "lo", "acc"))
        s_chain = sem("gnn_chain")
        with nc.Block() as block:
            @block.tensor
            def _(pe):
                for i in range(STEPS + 1):
                    if i:
                        pe.wait_ge(s_lo, NT * i)
                        pe.wait_ge(s_hi, NT * i)
                    else:
                        pe.wait_ge(s_in_w, 48)
                    for t in range(NT):
                        n = i * NT + t
                        if n >= 2:
                            pe.wait_ge(s_cur, n - 1)
                        if i == 0:
                            for k in range(KD):
                                mm = pe.matmul(PS[:, n % 2, :], xT[:, k, t * P:(t + 1) * P], W0[:, k, :],
                                               start=(k == 0), stop=(k == KD - 1))
                        else:
                            for j in range(NT):
                                for part in (hi, lo):
                                    mm = pe.matmul(PS[:, n % 2, :], adj[:, j, t * P:(t + 1) * P],
                                                   part[(i + 1) % 2][:, j, :], start=(j == 0 and part is hi),
                                                   stop=(j == NT - 1 and part is lo))
                        mm.then_inc(s_sum, 1)

            @block.scalar
            def _(act):
                for i in range(STEPS + 1):
                    for t in range(NT):
                        n = i * NT + t
                        if i:
                            act.wait_ge(s_sum, n + 1)
                            if n >= 2:
                                act.wait_ge(s_acc, n - 1)
                            act.activation(cur[:, n % 2, :], PS[:, n % 2, :], ACT.Copy,
                                           scale=rinv[:, t:t + 1]).then_inc(s_cur, 1)
                        act.wait_ge(s_cur, n + 1)
                        act.copy(hi[i % 2][:, t, :], cur[:, n % 2, :]).then_inc(s_hi, 1)

            @block.vector
            def _(dve):
                n_link = [0]

                def link(ins):
                    n_link[0] += 1
                    ins.then_inc(s_chain, 1)
                    dve.wait_ge(s_chain, n_link[0])

                for i in range(STEPS + 1):
                    for t in range(NT):
                        n = i * NT + t
                        if i == 0:
                            dve.wait_ge(s_sum, n + 1)
                            dve.tensor_tensor(cur[:, n % 2, :], PS[:, n % 2, :], b0[:], ALU.add
                                              ).then_inc(s_cur, 1)
                            dve.wait_ge(s_cur, n + 1)
                            link(dve.tensor_scalar(acc[:, t, :], cur[:, n % 2, :], wdiff[:, 0:1], None, ALU.mult))
                        else:
                            dve.wait_ge(s_cur, n + 1)
                            link(dve.scalar_tensor_tensor(acc[:, t, :], cur[:, n % 2, :], wdiff[:, i:i + 1],
                                                          acc[:, t, :], ALU.mult, ALU.add))
                        dve.wait_ge(s_hi, n + 1)
                        dve.tensor_tensor(lo[i % 2][:, t, :], cur[:, n % 2, :], hi[i % 2][:, t, :].bitcast(F32),
                                          ALU.subtract).then_inc(s_lo, 1)
                        if i == STEPS:
                            dve.scalar_tensor_tensor(x[:, t, :], acc[:, t, :], 0.0, x[:, t, :], ALU.max, ALU.add
                                                     ).then_inc(s_acc, 1)
                        else:
                            dve.wait_ge(s_lo, n + 1)
                            dve.sem_inc(s_acc, 1)

        def routing(name, X0, K, logits_w, bias_d, b2_d, flat, NB, slot_dram, xT, sb):
            s_w, s_log, s_logm, s_exp, s_pick = (sem(f"{name}_{k}") for k in ("w", "logits", "moved", "exp", "pick"))
            s_rank, s_slot, s_pad, s_padded, s_sc, s_back = (
                sem(f"{name}_{k}") for k in ("rank", "slot", "pad", "padded", "scattered", "listed"))
            s_chain, s_rd, s_done = sem(name + "_chain"), sem(name + "_rd"), sem(name + "_done")
            s_sw = sem(name + "_sw")
            s_tw, s_twm, s_ready = sem(name + "_tw"), sem(name + "_twm"), sem(name + "_ready")
            wg, bg, lg, top, idx = sb["wg"], sb["bg"], sb["lg"], sb["top"], sb["idx"]
            idxf, M, Mb, nm, sm, rm = sb["idxf"], sb["M"], sb["Mb"], sb["nm"], sb["sm"], sb["rm"]
            sw, swT, rnk, base, scr = sb["sw"], sb["swT"], sb["rnk"], sb["base"], sb["scr"]
            cnt, nb, cum, beg = sb["cnt"], sb["nb"], sb["cum"], sb["beg"]
            nbi, ri, bi, sl, sl2 = sb["nbi"], sb["ri"], sb["bi"], sb["sl"], sb["sl2"]
            lst, gat, pad, own, owni, b2s = sb["lst"], sb["gat"], sb["pad"], sb["own"], sb["owni"], sb["b2s"]
            LOGP = P.bit_length() - 1
            with nc.Block() as block:
                @block.sync
                def _(sp):
                    sp.dma_start(wg[:], logits_w.rearrange("(k p) n -> p k n", p=P)).then_inc(s_w, 16)
                    sp.dma_start(bg[:], bcast(bias_d, X0)).then_inc(s_w, 16)
                    sp.dma_start(b2s[:], b2_d).then_inc(s_w, 16)
                    sp.wait_ge(s_pad, 1)
                    sp.dma_start(slot_dram.rearrange("(p b) o -> p (b o)", p=P), pad[:]).then_inc(s_padded, 16)
                    sp.wait_ge(s_w, 48)
                    sp.wait_ge(s_sc, 16 * NT * K)
                    sp.dma_start(lst[:], slot_dram.rearrange("(p b) o -> p (b o)", p=P)).then_inc(s_back, 16)
                    sp.wait_ge(s_back, 16)

                @block.gpsimd
                def _(pool):
                    if K == 1:
                        pool.iota(sb["tok1"][:], [[P, NT]], 0, 1)
                    pool.memset(pad[:], NO_ROW).then_inc(s_pad, 1)
                    pool.wait_ge(s_padded, 16)
                    pool.wait_ge(s_slot, 1)
                    for t in range(NT):
                        for k in range(K):
                            pool.indirect_dma_start(
                                slot_dram, bass.IndirectOffsetOnAxis(sl2[:, t, k:k + 1], 0),
                                tokid[:, t, k:k + 1] if K > 1 else sb["tok1"][:, t:t + 1], None,
                            ).then_inc(s_sc, 16)

                @block.tensor
                def _(pe):
                    pe.wait_ge(s_w, 48)
                    for t in range(NT):
                        if t >= 2:
                            pe.wait_ge(s_logm, t - 1)
                        for k in range(KD):
                            mm = pe.matmul(PS[:, t % 2, 0:X0], xT[:, k, t * P:(t + 1) * P], wg[:, k, :],
                                           start=(k == 0), stop=(k == KD - 1))
                        mm.then_inc(s_log, 1)
                    pe.wait_ge(s_pick, 1)
                    for t in range(NT + 1):
                        o = PS[:, 2 + t // 8, (t % 8) * X0:(t % 8 + 1) * X0]
                        for j in range(min(t, NT)):
                            pe.matmul(o, onesb[:], Mb[:, j, :], start=(j == 0), stop=(t == NT and j == NT - 1))
                        if t < NT:
                            mm = pe.matmul(o, before[:], Mb[:, t, :], start=(t == 0), stop=True)
                    pe.matmul(PS[:, 4, 0:X0], onesb[:], zerob[:, 0:X0], start=True, stop=True).then_inc(s_rank, 1)
                    pe.wait_ge(s_sw, 1)
                    for t in range(NT):
                        mm = pe.transpose(PS[0:X0, 6 + t // 4, (t % 4) * P:(t % 4 + 1) * P], sw[:, t, :], ident[:])
                    mm.then_inc(s_tw, 1)

                @block.scalar
                def _(act):
                    if K == 1:
                        act.wait_ge(s_rd, 1)
                        act.activation(sb["gate"][:], sm[:], ACT.Exp).then_inc(s_done, 1)
                    for t in range(NT if K > 1 else 0):
                        act.wait_ge(s_ready, t + 1)
                        act.activation(lg[:, t, :], lg[:, t, :], ACT.Exp, bias=nm[:, t:t + 1],
                                       accum_out=sm[:, t:t + 1]).then_inc(s_exp, 1)
                    act.wait_ge(s_tw, 1)
                    act.copy(swT[:], PS[0:X0, 6:8, :].rearrange("p a n -> p (a n)")).then_inc(s_twm, 1)

                @block.vector
                def _(dve):
                    n = [0]

                    def link(ins):
                        n[0] += 1
                        ins.then_inc(s_chain, 1)
                        dve.wait_ge(s_chain, n[0])

                    dve.wait_ge(s_w, 48)
                    for t in range(NT):
                        dve.wait_ge(s_log, t + 1)
                        dve.tensor_tensor(lg[:, t, :], PS[:, t % 2, 0:X0], bg[:], ALU.add).then_inc(s_logm, 1)
                        dve.wait_ge(s_logm, t + 1)
                        link(dve.tensor_reduce(nm[:, t:t + 1], lg[:, t, :], X, ALU.max))
                        if K == 1:
                            link(dve.max(top[:, t, :], lg[:, t, :]))
                            link(dve.max_index(idx[:, t, :], top[:, t, :], lg[:, t, :]))
                        dve.tensor_scalar(nm[:, t:t + 1], nm[:, t:t + 1], -1.0, None, ALU.mult).then_inc(s_ready, 1)
                    for t in range(NT):
                        if K > 1:
                            dve.wait_ge(s_exp, t + 1)
                            link(dve.reciprocal(rm[:, t:t + 1], sm[:, t:t + 1]))
                            link(dve.tensor_scalar(lg[:, t, :], lg[:, t, :], rm[:, t:t + 1], None, ALU.mult))
                            link(dve.max(top[:, t, :], lg[:, t, :]))
                            link(dve.max_index(idx[:, t, :], top[:, t, :], lg[:, t, :]))
                    if K == 1:
                        dve.wait_ge(s_ready, NT)
                        dve.tensor_tensor(sm[:], top[:, :, 0], nm[:], ALU.add).then_inc(s_rd, 1)
                        dve.wait_ge(s_done, 1)
                        link(dve.reciprocal(rm[:], sb["gate"][:]))
                        link(dve.tensor_tensor(sb["gate"][:], sb["gate"][:], rm[:], ALU.mult))
                    link(dve.tensor_copy(idxf[:], idx[:, :, 0:K]))
                    for t in range(NT):
                        for k in range(K):
                            last = dve.tensor_scalar(M[:, t, k, :], iotaf[:, 0:X0], idxf[:, t, k:k + 1], None, ALU.is_equal)
                    if K > 1:
                        link(last)
                        dve.tensor_tensor(Mb[:], M[:, :, 0, :], M[:, :, 1, :], ALU.add).then_inc(s_pick, 1)
                        for t in range(NT):
                            link(dve.tensor_scalar(sw[:, t, :], M[:, t, 0, :], top[:, t, 0:1], None, ALU.mult))
                            link(dve.scalar_tensor_tensor(sw[:, t, :], M[:, t, 1, :], top[:, t, 1:2], sw[:, t, :],
                                                          ALU.mult, ALU.add))
                    else:
                        link(last)
                        link(dve.tensor_copy(sw[:], M[:, :, 0, :]))
                        dve.tensor_copy(Mb[:], M[:, :, 0, :]).then_inc(s_pick, 1)
                    dve.sem_inc(s_sw, 1)
                    dve.wait_ge(s_rank, 1)
                    link(dve.tensor_copy(cnt[:], PS[:, 3, 0:X0]))
                    if flat:
                        link(dve.tensor_scalar(nb[:], cnt[:], float(P - 1), None, ALU.add))
                    else:
                        link(dve.tensor_scalar(nb[:], cnt[:], -float(P), 0.0, ALU.add, ALU.max))
                        link(dve.tensor_scalar(nb[:], nb[:], float(P - 1), None, ALU.add))
                    link(dve.tensor_copy(nbi[:], nb[:]))
                    link(dve.tensor_scalar(nbi[:], nbi[:], LOGP, None, ALU.logical_shift_right))
                    link(dve.tensor_copy(nb[:], nbi[:]))
                    link(dve.tensor_tensor_scan(cum[:], nb[:], nb[:], 0.0, ALU.add, ALU.bypass))
                    link(dve.tensor_tensor(beg[:], cum[:], nb[:], ALU.subtract))
                    for t in range(NT):
                        for k in range(K):
                            link(dve.tensor_tensor_reduce(scr[:], M[:, t, k, :], PS[:, 2, t * X0:(t + 1) * X0], 1.0, 0.0,
                                                          ALU.mult, ALU.add, rnk[:, t, k:k + 1]))
                            link(dve.tensor_tensor_reduce(scr[:], M[:, t, k, :], beg[:], 1.0, 0.0,
                                                          ALU.mult, ALU.add, base[:, t, k:k + 1]))
                    rf, bf, sf = (a[:].rearrange("p t k -> p (t k)") for a in (rnk, base, sl))
                    idf = idxf[:].rearrange("p t k -> p (t k)")
                    rif, bif = (a[:].rearrange("p t k -> p (t k)") for a in (ri, bi))
                    link(dve.tensor_copy(rif, rf))
                    link(dve.tensor_scalar(bif, rif, LOGP, None, ALU.logical_shift_right))
                    link(dve.tensor_scalar(rif, rif, P - 1, None, ALU.bitwise_and))
                    link(dve.tensor_copy(rf, rif))
                    link(dve.tensor_copy(sf, bif))
                    if flat:
                        link(dve.tensor_tensor(sf, sf, bf, ALU.add))
                    else:
                        tmp = sb["tmp"][:].rearrange("p t k -> p (t k)")
                        link(dve.tensor_tensor(bf, bf, sf, ALU.add))
                        link(dve.tensor_scalar(bf, bf, float(X0 - 1), None, ALU.add))
                        link(dve.tensor_scalar(tmp, sf, 0.0, None, ALU.is_equal))
                        link(dve.tensor_tensor(sf, idf, bf, ALU.subtract))
                        link(dve.tensor_tensor(sf, sf, tmp, ALU.mult))
                        link(dve.tensor_tensor(sf, sf, bf, ALU.add))
                    link(dve.scalar_tensor_tensor(sf, rf, float(NB), sf, ALU.mult, ALU.add))
                    dve.tensor_copy(sl2[:], sl[:]).then_inc(s_slot, 1)
                    NO = NB if flat else NB - X0
                    for j in range(NO):
                        link(dve.tensor_scalar(scr[:], cum[:], float(j), None, ALU.is_le, ALU.add,
                                               accum_out=own[:, j:j + 1]))
                    link(dve.tensor_scalar(own[:, 0:NO], own[:, 0:NO], float(X0 - 1), None, ALU.min))
                    dve.tensor_copy(own[:, NO:NO + 1], cum[:, X0 - 1:X0]).then_inc(s_chain, 1)
                    n[0] += 1
                    dve.wait_ge(s_chain, n[0])
                    link(dve.tensor_copy(owni[:], own[:]))
                    dve.wait_ge(s_back, 16)
                    if K > 1:
                        link(dve.tensor_scalar(gat[:], lst[:], 1, None, ALU.logical_shift_right))

        def router_buffers(tag, X0, K, NB, flat, at):
            names = dict(
                wg=([P, KD, X0], F32), bg=([P, X0], F32), lg=([P, NT, X0], F32), top=([P, NT, 8], F32),
                idx=([P, NT, 8], U32), idxf=([P, NT, K], F32), M=([P, NT, K, X0], F32), Mb=([P, NT, X0], BF16),
                nm=([P, NT], F32), sm=([P, NT], F32), rm=([P, NT], F32), sw=([P, NT, X0], F32),
                swT=([X0, N], F32), rnk=([P, NT, K], F32), base=([P, NT, K], F32), scr=([P, X0], F32),
                cnt=([P, X0], F32), nb=([P, X0], F32), cum=([P, X0], F32), beg=([P, X0], F32),
                nbi=([P, X0], I32), ri=([P, NT, K], I32), bi=([P, NT, K], I32), sl=([P, NT, K], F32),
                sl2=([P, NT, K], I32), tmp=([P, NT, K], F32), lst=([P, NB], I32), gat=([P, NB], I32),
                pad=([P, NB], I32), own=([P, 17], F32), owni=([P, 17], I32), b2s=([X0, D], F32),
                tok1=([P, NT], I32), gate=([P, NT], F32))
            if not flat:
                names["own"] = ([P, NB - X0 + 1], F32)
                names["owni"] = ([P, NB - X0 + 1], I32)
            else:
                names["own"] = ([P, NB + 1], F32)
                names["owni"] = ([P, NB + 1], I32)
            made = {}
            for k, (shape, dt) in names.items():
                size = 2 if dt == BF16 else 4
                for s in shape[1:]:
                    size *= s
                made[k] = place(f"{tag}_{k}", shape, dt, at)
                at += (size + 31) // 32 * 32
            made["end"] = at
            return made

        r0 = router_buffers("r0", NX0, TOPK, NB0, False, 176 * KIB)
        assert r0["end"] <= ARENA, r0["end"]
        phase()
        layernorm("ln1", x, xln, xT, keep=True)
        phase()
        routing("rt0", NX0, TOPK, ins["L0_ffn_Wg"], ins["L0_ffn_bg"], ins["L0_ffn_b2"], False, NB0, slot0_dram,
                xT, r0)

        w1r = place("w1r", [P, 4, KD, H], F32, 112 * KIB)
        w2r = place("w2r", [P, 4, HC, D], F32, 128 * KIB)
        xg = place("xg", [P, 4, D], F32, 144 * KIB)
        xgT = place("xgT", [P, 2, KD, P], F32, 152 * KIB)
        hT = place("hT", [P, 2, HC, P], F32, 156 * KIB)
        yo = place("yo", [P, 4, D], F32, 158 * KIB)
        b1T = place("b1T", [P, HC, NX0], F32, 166 * KIB)
        b1s = place("b1s", [NX0, H], F32, 167 * KIB)
        gi = place("gi", [P, 4, 8], I32, 168 * KIB)
        si = place("si", [P, 4, 8], I32, 168 * KIB + 128)
        lst, gat, owni = r0["lst"], r0["gat"], r0["owni"]

        def wait(eng, s, v):
            if not isinstance(v, int) or v > 0:
                eng.wait_ge(s, v)

        def loop(eng, body):
            for j in range(4):
                body(j, 0, j, False)
            with eng.Fori(1, NX0 // 4 - 1) as g:
                for j in range(4):
                    body(eng.snap(g * 4 + j), g, j, False)
            for j in range(4):
                body(NX0 - 4 + j, NX0 // 4 - 1, j, j == 3)

        phase()
        s_w = [sem(f"x0_w{j}") for j in range(4)]
        s_xg = [sem(f"x0_xg{j}") for j in range(4)]
        s_ys = [sem(f"x0_ys{j}") for j in range(4)]
        s_t, s_tm, s_h, s_hm, s_y, s_ym = (sem("x0_" + k) for k in ("t", "tm", "h", "hm", "y", "ym"))
        s_pass = sem("x0_pass")
        s_b1, s_b1t, s_b1m, s_clear, s_gi = (sem("x0_" + k) for k in ("b1", "b1t", "b1m", "clear", "gi"))
        with nc.Block() as block:
            @block.sync
            def _(sp):
                sp.dma_start(b1s[:], ins["L0_ffn_b1"]).then_inc(s_b1, 16)

                def body(e, g, j, last):
                    wait(sp, s_y, e - 3)
                    one = slice(e, e + 1) if isinstance(e, int) else bass.ds(e, 1)
                    sp.dma_start(w1r[:, j, :, :], ins["L0_ffn_W1"][one].rearrange("o (k p) h -> p (o k) h", p=P)
                                 ).then_inc(s_w[j], 16)
                    sp.dma_start(w2r[:, j, :, :], ins["L0_ffn_W2"][one].rearrange("o (k p) h -> p (o k) h", p=P)
                                 ).then_inc(s_w[j], 16)

                loop(sp, body)

            @block.gpsimd
            def _(pool):
                pool.memset(xg[:], 0.0).then_inc(s_clear, 1)
                pool.wait_ge(s_clear, 1)

                def fetch(e, g, j, n):
                    col = slice(e, e + 1) if isinstance(e, int) else bass.ds(e, 1)
                    wait(pool, s_t, e - 3)
                    pool.sem_inc(s_pass, 1)
                    pool.tensor_copy(gi[:, j, 0:1], gat[:, col]).then_inc(s_gi, 1)
                    pool.wait_ge(s_gi, n)
                    pool.sem_inc(s_pass, 1)
                    pool.indirect_dma_start(xg[:, j, :], None, xrow_dram,
                                            bass.IndirectOffsetOnAxis(gi[:, j, 0:1], 0), bounds_check=N - 1,
                                            oob_is_err=False).then_inc(s_xg[j], 16)

                def store(e, g, j, n):
                    col = slice(e, e + 1) if isinstance(e, int) else bass.ds(e, 1)
                    pool.wait_ge(s_ym, e + 1)
                    pool.sem_inc(s_pass, 1)
                    pool.tensor_copy(si[:, j, 0:1], lst[:, col]).then_inc(s_gi, 1)
                    pool.wait_ge(s_gi, n)
                    pool.sem_inc(s_pass, 1)
                    pool.indirect_dma_start(y_dram, bass.IndirectOffsetOnAxis(si[:, j, 0:1], 0), yo[:, j, :], None,
                                            bounds_check=N * TOPK - 1, oob_is_err=False).then_inc(s_ys[j], 16)

                def body(e, g, j, last):
                    if isinstance(e, int) and e < 3:
                        fetch(e, g, j, e + 1)
                        return
                    fetch(e, g, j, e * 2 - 2)
                    e3 = e - 3 if isinstance(e, int) else within(pool.snap(e - 3), 0, NX0 - 1)
                    store(e3, g, (j + 1) % 4, e * 2 - 1)

                loop(pool, body)
                for k in range(3):
                    e = NX0 - 3 + k
                    store(e, None, e % 4, 2 * NX0 - 2 + k)
                for j in range(4):
                    pool.wait_ge(s_ys[j], 16 * (NX0 // 4))
                pool.wait_ge(s_pass, 4 * NX0)

            @block.tensor
            def _(pe):
                pe.wait_ge(s_b1, 16)
                for c in range(HC):
                    mm = pe.transpose(PS[:, 6, c * NX0:(c + 1) * NX0], b1s[:, c * P:(c + 1) * P],
                                      ident[0:NX0, 0:NX0])
                mm.then_inc(s_b1t, 1)

                def turn(e, g, j):
                    pe.wait_ge(s_xg[j], (g + 1) * 16)
                    wait(pe, s_tm, e - 1)
                    for k in range(KD):
                        mm = pe.transpose(PS[:, j % 2, k * P:(k + 1) * P], xg[:, j, k * P:(k + 1) * P], ident[:])
                    mm.then_inc(s_t, 1)

                def hidden(e, g, j):
                    pe.wait_ge(s_w[j], (g + 1) * 32)
                    pe.wait_ge(s_tm, e + 1)
                    wait(pe, s_hm, e - 1)
                    for c in range(HC):
                        for k in range(KD):
                            mm = pe.matmul(PS[:, 2 + j % 2, c * P:(c + 1) * P], w1r[:, j, k, c * P:(c + 1) * P],
                                           xgT[:, j % 2, k, :], start=(k == 0), stop=(k == KD - 1))
                    mm.then_inc(s_h, 1)

                def output(e, j):
                    pe.wait_ge(s_hm, e + 1)
                    wait(pe, s_ym, e - 1)
                    for c in range(HC):
                        mm = pe.matmul(PS[:, 4 + j % 2, :], hT[:, j % 2, c, :], w2r[:, j, c, :],
                                       start=(c == 0), stop=(c == HC - 1))
                    mm.then_inc(s_y, 1)

                turn(0, 0, 0)

                def body(e, g, j, last):
                    if not last:
                        turn(e + 1, g + 1 if j == 3 else g, (j + 1) % 4)
                    hidden(e, g, j)
                    if not (isinstance(e, int) and e == 0):
                        output(e - 1, (j + 3) % 4)

                loop(pe, body)
                output(NX0 - 1, 3)

            @block.scalar
            def _(act):
                act.wait_ge(s_b1t, 1)
                act.copy(b1T[:].rearrange("p c e -> p (c e)"), PS[:, 6, 0:HC * NX0]).then_inc(s_b1m, 1)
                act.wait_ge(s_b1m, 1)

                def body(e, g, j, last):
                    col = slice(e, e + 1) if isinstance(e, int) else bass.ds(e, 1)
                    act.wait_ge(s_h, e + 1)
                    wait(act, s_y, e - 1)
                    for c in range(HC):
                        a = act.activation(hT[:, j % 2, c, :], PS[:, 2 + j % 2, c * P:(c + 1) * P], ACT.Relu,
                                           bias=b1T[:, c, col])
                    a.then_inc(s_hm, 1)

                loop(act, body)

            @block.vector
            def _(dve):
                def turned(e, j):
                    dve.wait_ge(s_t, e + 1)
                    wait(dve, s_h, e - 1)
                    dve.tensor_copy(xgT[:, j % 2, :, :].rearrange("p k n -> p (k n)"), PS[:, j % 2, :]
                                    ).then_inc(s_tm, 1)

                def moved(e, g, j):
                    dve.wait_ge(s_y, e + 1)
                    wait(dve, s_ys[j], g * 16)
                    dve.tensor_copy(yo[:, j, :], PS[:, 4 + j % 2, :]).then_inc(s_ym, 1)

                turned(0, 0)

                def body(e, g, j, last):
                    if not last:
                        turned(e + 1, (j + 1) % 4)
                    if not (isinstance(e, int) and e == 0):
                        moved(e - 1, g if j else g - 1, (j + 3) % 4)

                loop(dve, body)
                moved(NX0 - 1, NX0 // 4 - 1, 3)

        NO0 = NB0 - NX0
        phase()
        s_pass = sem("x1_pass")
        s_next, s_w, s_xg, s_ys, s_gi = (sem("x1_" + k) for k in ("next", "w", "xg", "ys", "gi"))
        s_t, s_tm, s_h, s_hm, s_y, s_ym = (sem("x1_" + k) for k in ("t", "tm", "h", "hm", "y", "ym"))
        with nc.Block() as block:
            def each(eng, body):
                more = eng.value_load(owni[0:1, NO0:NO0 + 1], min_val=0, max_val=NO0)
                with eng.If(more > 0):
                    with eng.Fori(0, more) as j:
                        eng.wait_ge(s_next, j + 1)
                        body(j)

            @block.sync
            def _(sp):
                def body(j):
                    e = sp.value_load(owni[0:1, bass.ds(j, 1)], min_val=0, max_val=NX0 - 1)
                    sp.dma_start(w1r[:, 0, :, :], ins["L0_ffn_W1"][bass.ds(e, 1)].rearrange(
                        "o (k p) h -> p (o k) h", p=P)).then_inc(s_w, 16)
                    sp.dma_start(w2r[:, 0, :, :], ins["L0_ffn_W2"][bass.ds(e, 1)].rearrange(
                        "o (k p) h -> p (o k) h", p=P)).then_inc(s_w, 16)

                each(sp, body)

            @block.gpsimd
            def _(pool):
                pool.sem_inc(s_next, 1)

                def body(j):
                    col = bass.ds(within(pool.snap(j + NX0), NX0, NB0 - 1), 1)
                    pool.tensor_copy(gi[:, 0, 0:1], gat[:, col])
                    pool.tensor_copy(si[:, 0, 0:1], lst[:, col]).then_inc(s_gi, 1)
                    pool.wait_ge(s_gi, j + 1)
                    pool.sem_inc(s_pass, 1)
                    pool.indirect_dma_start(xg[:, 0, :], None, xrow_dram,
                                            bass.IndirectOffsetOnAxis(gi[:, 0, 0:1], 0), bounds_check=N - 1,
                                            oob_is_err=False).then_inc(s_xg, 16)
                    pool.wait_ge(s_ym, j + 1)
                    pool.sem_inc(s_pass, 1)
                    pool.indirect_dma_start(y_dram, bass.IndirectOffsetOnAxis(si[:, 0, 0:1], 0), yo[:, 0, :], None,
                                            bounds_check=N * TOPK - 1, oob_is_err=False).then_inc(s_ys, 16)
                    pool.wait_ge(s_ys, (j + 1) * 16)
                    pool.sem_inc(s_next, 1)

                each(pool, body)

            @block.tensor
            def _(pe):
                def body(j):
                    pe.wait_ge(s_xg, (j + 1) * 16)
                    for k in range(KD):
                        mm = pe.transpose(PS[:, 0, k * P:(k + 1) * P], xg[:, 0, k * P:(k + 1) * P], ident[:])
                    mm.then_inc(s_t, 1)
                    pe.wait_ge(s_w, (j + 1) * 32)
                    pe.wait_ge(s_tm, j + 1)
                    for c in range(HC):
                        for k in range(KD):
                            mm = pe.matmul(PS[:, 2, c * P:(c + 1) * P], w1r[:, 0, k, c * P:(c + 1) * P],
                                           xgT[:, 0, k, :], start=(k == 0), stop=(k == KD - 1))
                    mm.then_inc(s_h, 1)
                    pe.wait_ge(s_hm, j + 1)
                    for c in range(HC):
                        mm = pe.matmul(PS[:, 4, :], hT[:, 0, c, :], w2r[:, 0, c, :], start=(c == 0),
                                       stop=(c == HC - 1))
                    mm.then_inc(s_y, 1)

                each(pe, body)

            @block.scalar
            def _(act):
                def body(j):
                    e = act.value_load(owni[0:1, bass.ds(j, 1)], min_val=0, max_val=NX0 - 1)
                    act.wait_ge(s_h, j + 1)
                    for c in range(HC):
                        a = act.activation(hT[:, 0, c, :], PS[:, 2, c * P:(c + 1) * P], ACT.Relu,
                                           bias=b1T[:, c, bass.ds(e, 1)])
                    a.then_inc(s_hm, 1)

                each(act, body)

            @block.vector
            def _(dve):
                def body(j):
                    dve.wait_ge(s_t, j + 1)
                    dve.tensor_copy(xgT[:, 0, :, :].rearrange("p k n -> p (k n)"), PS[:, 0, :]).then_inc(s_tm, 1)
                    dve.wait_ge(s_y, j + 1)
                    dve.tensor_copy(yo[:, 0, :], PS[:, 4, :]).then_inc(s_ym, 1)

                each(dve, body)

        yb = place("yb", [P, 2, TOPK, D], F32, 112 * KIB)
        o0 = place("o0", [P, NT, D], F32, 120 * KIB)
        gamma = place("gamma", [P, D], F32, 136 * KIB)
        beta = place("beta", [P, D], F32, 138 * KIB)
        phase()
        s_yb, s_gb = [sem("c0_yb0"), sem("c0_yb1")], sem("c0_gb")
        s_bias, s_sum, s_stat, s_sqrt, s_chain = (sem("c0_" + k) for k in ("bias", "sum", "stat", "sqrt", "chain"))
        with nc.Block() as block:
            @block.sync
            def _(sp):
                sp.dma_start(gamma[:], bcast(ins["L0_ffn_gamma"], D)).then_inc(s_gb, 16)
                sp.dma_start(beta[:], bcast(ins["L0_ffn_beta"], D)).then_inc(s_gb, 16)
                for t in range(NT):
                    if t >= 2:
                        sp.wait_ge(s_sum, t - 1)
                    sp.dma_start(yb[:, t % 2, :, :], y_dram.rearrange("(t p k) d -> t p k d", p=P, k=TOPK)[t]
                                 ).then_inc(s_yb[t % 2], 16)

            @block.tensor
            def _(pe):
                for t in range(NT):
                    if t >= 4:
                        pe.wait_ge(s_sum, t - 3)
                    pe.matmul(PS[:, t % 4, :], r0["swT"][:, t * P:(t + 1) * P], r0["b2s"][:], start=True,
                              stop=True).then_inc(s_bias, 1)

            @block.scalar
            def _(act):
                act.wait_ge(s_stat, 1)
                act.activation(sq[:], ve[:], ACT.Sqrt).then_inc(s_sqrt, 1)

            @block.vector
            def _(dve):
                n = [0]

                def link(ins):
                    n[0] += 1
                    ins.then_inc(s_chain, 1)
                    dve.wait_ge(s_chain, n[0])

                top = r0["top"]
                for t in range(NT):
                    dve.wait_ge(s_bias, t + 1)
                    dve.wait_ge(s_yb[t % 2], 16 * (t // 2 + 1))
                    link(dve.tensor_tensor(o0[:, t, :], PS[:, t % 4, :], xln[:, t, :], ALU.add))
                    link(dve.scalar_tensor_tensor(o0[:, t, :], yb[:, t % 2, 0, :], top[:, t, 0:1], o0[:, t, :],
                                                  ALU.mult, ALU.add))
                    dve.scalar_tensor_tensor(o0[:, t, :], yb[:, t % 2, 1, :], top[:, t, 1:2], o0[:, t, :],
                                             ALU.mult, ALU.add).then_inc(s_sum, 1)
                    dve.wait_ge(s_sum, t + 1)
                    link(dve.bn_stats(st[:, t, :], o0[:, t, :]))
                    last = dve.bn_aggr(mv[:, t, :], st[:, t, :])
                link(last)
                dve.tensor_scalar(ve[:], mv[:, :, 1], LN_EPS, None, ALU.add).then_inc(s_stat, 1)
                dve.wait_ge(s_sqrt, 1)
                link(dve.reciprocal(tq[:], sq[:]))
                link(dve.tensor_tensor(tq[:], tq[:], ve[:], ALU.mult))
                link(dve.tensor_tensor(tq[:], tq[:], sq[:], ALU.add))
                link(dve.tensor_scalar(tq[:], tq[:], 0.5, None, ALU.mult))
                link(dve.reciprocal(rs[:], tq[:]))
                dve.wait_ge(s_gb, 32)
                for t in range(NT):
                    last = dve.tensor_scalar(o0[:, t, :], o0[:, t, :], mv[:, t, 0:1], rs[:, t:t + 1],
                                             ALU.subtract, ALU.mult)
                link(last)
                for t in range(NT):
                    last = dve.tensor_tensor(o0[:, t, :], o0[:, t, :], gamma[:], ALU.mult)
                link(last)
                for t in range(NT):
                    last = dve.tensor_tensor(o0[:, t, :], o0[:, t, :], beta[:], ALU.add)
                link(last)
                for t in range(NT):
                    last = dve.tensor_tensor(x[:, t, :], x[:, t, :], o0[:, t, :], ALU.add)
                link(last)

        a_bc = place("a_bc", [P, HEADS, N], F32, 161 * KIB)
        bsb = place("bsb", [P, NT, HEADS], F32, 101 * KIB + 640)
        x2T = place("x2T", [P, KF, N], F32, 16 * KIB)

        def project(tag, KI, CH, xT, W, W_d, att_src, att_dst, h, v, adr):
            F = HEADS * CH
            FB = F // 512
            att = place(tag + "_att", [P, 2, F], F32, 193 * KIB)
            prod = place(tag + "_prod", [P, F], F32, 201 * KIB)
            aTs = place(tag + "_aTs", [2 * HEADS, N], F32, 201 * KIB)
            s_in, s_att, s_v, s_h, s_hm, s_a, s_am, s_b, s_row, s_bc = (
                sem(f"{tag}_{k}") for k in ("in", "att", "v", "h", "hm", "a", "am", "b", "row", "bc"))
            s_ones, s_chain, s_bm = sem(tag + "_ones"), sem(tag + "_chain"), sem(tag + "_bm")
            with nc.Block() as block:
                @block.sync
                def _(sp):
                    sp.dma_start(W[:], W_d.rearrange("(k p) n -> p k n", p=P)).then_inc(s_in, 16)
                    for n, a in enumerate((att_src, att_dst)):
                        sp.dma_start(att[:, n, :], bcast(a.rearrange("h c -> (h c)"), F)).then_inc(s_att, 16)
                    sp.wait_ge(s_am, 1)
                    sp.dma_start(adr, aTs[:]).then_inc(s_row, 16)
                    sp.wait_ge(s_row, 16)
                    sp.dma_start(a_bc[:].rearrange("p h n -> p (h n)"), bcast(adr[0:HEADS, :].rearrange("h n -> (h n)"),
                                                                              HEADS * N)).then_inc(s_bc, 16)
                    sp.wait_ge(s_bc, 16)

                @block.gpsimd
                def _(pool):
                    pool.memset(h[:, :, :, CH:CH + 1], 1.0).then_inc(s_ones, 1)

                @block.vector
                def _(dve):
                    n = [0]

                    def link(ins):
                        n[0] += 1
                        ins.then_inc(s_chain, 1)
                        dve.wait_ge(s_chain, n[0])

                    dve.wait_ge(s_in, 16)
                    dve.wait_ge(s_att, 32)
                    for k in range(KI):
                        for a in range(2):
                            link(dve.tensor_tensor(prod[:], W[:, k, :], att[:, a, :], ALU.mult))
                            link(dve.tensor_reduce(v[:, k, a * HEADS:(a + 1) * HEADS],
                                                   prod[:].rearrange("p (h c) -> p h c", h=HEADS), X, ALU.add))
                    dve.sem_inc(s_v, 1)
                    dve.wait_ge(s_b, 1)
                    dve.tensor_copy(bsb[:].rearrange("p t h -> p (t h)"), PS[:, 6, 0:NT * HEADS]).then_inc(s_bm, 1)

                @block.tensor
                def _(pe):
                    pe.wait_ge(s_in, 16)
                    for t in range(NT):
                        if t >= 2:
                            pe.wait_ge(s_hm, t - 1)
                        for f in range(FB):
                            for k in range(KI):
                                mm = pe.matmul(PS[:, 2 * (t % 2) + f, :], xT[:, k, t * P:(t + 1) * P],
                                               W[:, k, f * 512:(f + 1) * 512], start=(k == 0), stop=(k == KI - 1))
                        mm.then_inc(s_h, 1)
                    pe.wait_ge(s_v, 1)
                    for half in range(2):
                        for k in range(KI):
                            mm = pe.matmul(PS[0:2 * HEADS, 4 + half, :], v[:, k, :], xT[:, k, half * 512:(half + 1) * 512],
                                           start=(k == 0), stop=(k == KI - 1))
                    mm.then_inc(s_a, 1)
                    for t in range(NT):
                        for k in range(KI):
                            mm = pe.matmul(PS[:, 6, t * HEADS:(t + 1) * HEADS], xT[:, k, t * P:(t + 1) * P],
                                           v[:, k, HEADS:2 * HEADS], start=(k == 0), stop=(k == KI - 1))
                    mm.then_inc(s_b, 1)

                @block.scalar
                def _(act):
                    for t in range(NT):
                        act.wait_ge(s_h, t + 1)
                        act.copy(h[:, t, :, 0:CH], PS[:, 2 * (t % 2):2 * (t % 2) + FB, :].rearrange(
                            "p a (h c) -> p (a h) c", c=CH)).then_inc(s_hm, 1)
                    act.wait_ge(s_a, 1)
                    act.copy(aTs[:], PS[0:2 * HEADS, 4:6, :].rearrange("p a n -> p (a n)")).then_inc(s_am, 1)

        am = place("am", [P, 4, N], F32, 145 * KIB)
        r4 = place("r4", [P, 2, N], F32, 102 * KIB)
        PTr = place("PTr", [P, 2, NT, P], F32, 197 * KIB)
        mt = place("mt", [P, N], BF16, 96 * KIB)
        negm = place("negm", [P, 4], F32, 101 * KIB + 896)
        mrow = place("mrow", [P, 4], F32, 101 * KIB + 928)
        m2 = place("m2", [P, 4], F32, 101 * KIB + 960)
        den = place("den", [P, 2], F32, 101 * KIB + 992)
        bsb4 = place("bsb4", [P, NT, HEADS], F32, 144 * KIB + 608)
        q2 = place("q2", [P, 4], F32, 144 * KIB + 544)
        spare = place("spare", [P, HEADS], F32, 144 * KIB + 512)

        def attend(tag, CH, h, bias_d, final):
            F = HEADS * CH
            bias = place(tag + "_bias", [P, F], F32, 193 * KIB)
            o = [place(f"{tag}_o{k}", [P, 4, CH], F32, at) for k, at in enumerate((110 * KIB, 205 * KIB))]
            if final:
                ot = place(tag + "_ot", [P, HEADS, CH], F32, 110 * KIB)
                zt = place(tag + "_zt", [P, F], F32, 205 * KIB)
            s_bias, s_am, s_pre, s_exp, s_T, s_pt, s_O, s_ev = (
                sem(f"{tag}_{k}") for k in ("bias", "am", "pre", "exp", "T", "pt", "O", "ev"))
            s_sum, s_q2 = sem(tag + "_sum"), sem(tag + "_q2")
            s_ob, s_xt, s_xm, s_z, s_ze, s_ln, s_chain, s_mt = (
                sem(f"{tag}_{k}") for k in ("ob", "xt", "xm", "z", "ze", "ln", "chain", "mt"))

            def units(eng, step, tail):
                for hd in range(HEADS):
                    step(0, hd)
                with eng.Fori(1, NT) as t:
                    for hd in range(HEADS):
                        step(t, hd)
                for k in range(tail):
                    step(NT, k)

            def back(t, hd, lag):
                if hd >= lag:
                    return t, hd - lag
                if isinstance(t, int) and t == 0:
                    return None
                return t - 1, hd - lag + HEADS

            def done(t):
                return isinstance(t, int) and t >= NT

            with nc.Block() as block:
                @block.sync
                def _(sp):
                    sp.dma_start(bias[:], bcast(bias_d, F)).then_inc(s_bias, 16)

                @block.vector
                def _(dve):
                    state = {"k": 0}

                    def link(ins, t):
                        state["k"] += 1
                        ins.then_inc(s_chain, 1)
                        dve.wait_ge(s_chain, state["base"] + state["k"])

                    def masked(t, hd):
                        n = t * HEADS + hd
                        if hd == 0:
                            link(dve.tensor_copy(mt[:], mask[:, t, :] if isinstance(t, int)
                                                 else mask[:, bass.ds(t, 1), :].rearrange("p o n -> p (o n)")), t)
                        wait(dve, s_T, n - 3)
                        dve.memset(spare[:, hd:hd + 1], 0.0)
                        dve.tensor_tensor_reduce(am[:, hd % 4, :], a_bc[:, hd, :], mt[:], 1.0, -3.0e38, ALU.add,
                                                        ALU.max, mrow[:, hd % 4:hd % 4 + 1]).then_inc(s_am, 1)
                        if hd % 2 == 0:
                            return
                        two = slice(hd % 4 - 1, hd % 4 + 1)
                        dve.wait_ge(s_am, n + 1)
                        b = bsb[:, t, hd - 1:hd + 1] if isinstance(t, int) else \
                            bsb[:, bass.ds(t, 1), hd - 1:hd + 1].rearrange("p o n -> p (o n)")
                        link(dve.tensor_tensor(mrow[:, two], mrow[:, two], b, ALU.add), t)
                        link(dve.tensor_scalar(m2[:, two], mrow[:, two], -NEG_SLOPE, None, ALU.mult), t)
                        link(dve.scalar_tensor_tensor(negm[:, two], mrow[:, two], -1.0, m2[:, two], ALU.mult,
                                                      ALU.min), t)
                        dve.scalar_tensor_tensor(q2[:, two], b, NEG_SLOPE, negm[:, two], ALU.mult, ALU.add
                                                 ).then_inc(s_q2, 2)

                    def counted(t, hd, T):
                        n = t * HEADS + hd
                        dve.wait_ge(s_T, n + 1)
                        wait(dve, s_O, n - 1)
                        cols = slice(t * P, (t + 1) * P) if isinstance(t, int) else bass.ds(t * P, P)
                        dve.tensor_tensor(PTr[:, hd % 2, :, :],
                                          PS[:, 2 * (hd % 2):2 * (hd % 2) + 2, :].rearrange("p a (s d) -> p (a s) d", d=P),
                                          CT[:, :, cols], ALU.mult).then_inc(s_pt, 1)

                    def normed(t, hd, T):
                        n = t * HEADS + hd
                        dve.wait_ge(s_O, n + 1)
                        b = PS[:, 4 + hd % 2, :]
                        link(dve.tensor_scalar(den[:, 0:1], b[:, CH:CH + 1], 1e-16, None, ALU.add), T)
                        link(dve.reciprocal(den[:, 1:2], den[:, 0:1]), T)
                        if final:
                            dst = ot[:, hd, :]
                        else:
                            dve.wait_ge(s_xt, 2 * t + 1 + hd // 4)
                            dst = o[hd // 4][:, hd % 4, :]
                        dve.tensor_scalar(dst, b[:, 0:CH], den[:, 1:2], None, ALU.mult).then_inc(s_ev, 1)

                    def logsoftmax(t, T):
                        dve.wait_ge(s_ev, HEADS * (t + 1))
                        if not (isinstance(t, int) and t == 0):
                            dve.wait_ge(s_ze, t)
                        link(dve.tensor_tensor(zt[:], ot[:].rearrange("p h c -> p (h c)"), bias[:], ALU.add), T)
                        one = slice(t, t + 1) if isinstance(t, int) else bass.ds(t, 1)
                        link(dve.tensor_reduce(nmt[:, 0:1], zt[:], X, ALU.max), T)
                        link(dve.tensor_scalar(zt[:], zt[:], nmt[:, 0:1], None, ALU.subtract), T)
                        xr = x[:, one, :].rearrange("p o d -> p (o d)")
                        dve.tensor_tensor(xr, xr, zt[:], ALU.add).then_inc(s_z, 1)

                    def step(t, hd):
                        if hd == 0:
                            state["k"] = 0
                            state["base"] = dve_base(t)
                        if not done(t):
                            masked(t, hd)
                        if (u := back(t, hd, 3)) and not (done(t) and hd >= 3):
                            counted(*u, t)
                        if (u := back(t, hd, 4)) and not (done(t) and hd >= 4):
                            normed(*u, t)
                            if final and u[1] == HEADS - 1:
                                logsoftmax(u[0], t)

                    full = 1 + 3 * (HEADS // 2) + 2 * HEADS + (3 if final else 0)
                    head = full - 2 * 4 - (3 if final else 0)

                    def dve_base(t):
                        if isinstance(t, int) and t == 0:
                            return 0
                        return head + (t - 1) * full

                    dve.wait_ge(s_bias, 16)
                    dve.tensor_scalar(bsb4[:], bsb[:], 1 / NEG_SLOPE - 1, None, ALU.mult).then_inc(s_mt, 1)
                    units(dve, step, 4)
                    if final:
                        dve.wait_ge(s_ln, 1)
                        dve.wait_ge(s_z, NT)
                        for t in range(NT):
                            last = dve.tensor_scalar(x[:, t, :], x[:, t, :], ve[:, t:t + 1], None, ALU.subtract)
                        last.then_inc(s_z, 1)
                        dve.wait_ge(s_z, NT + 1)

                @block.scalar
                def _(act):
                    def weigh(t, hd):
                        n = t * HEADS + hd
                        act.wait_ge(s_am, n + 1)
                        wait(act, s_sum, n - 1)
                        b = bsb4[:, t, hd:hd + 1] if isinstance(t, int) else \
                            bsb4[:, bass.ds(t, 1), hd:hd + 1].rearrange("p o n -> p (o n)")
                        act.activation(r4[:, hd % 2, :], am[:, hd % 4, :], ACT.Relu, bias=b, scale=1 / NEG_SLOPE - 1
                                       ).then_inc(s_pre, 1)

                    def expd(t, hd):
                        act.wait_ge(s_q2, t * HEADS + hd + 1)
                        act.wait_ge(s_sum, t * HEADS + hd + 1)
                        act.activation(am[:, hd % 4, :], am[:, hd % 4, :], ACT.Exp, bias=q2[:, hd % 4:hd % 4 + 1],
                                       scale=NEG_SLOPE).then_inc(s_exp, 1)

                    def step(t, hd):
                        if not done(t):
                            weigh(t, hd)
                        if (u := back(t, hd, 1)) and not (done(t) and hd >= 1):
                            expd(*u)
                        if not final and hd in (4, 7) and not (isinstance(t, int) and t == 0):
                            half = 0 if hd == 4 else 1
                            act.wait_ge(s_xt, 2 * t + 1 + half)
                            cols = slice((t - 1) * P, t * P) if isinstance(t, int) else bass.ds((t - 1) * P, P)
                            act.activation(x2T[:, 4 * half:4 * half + 4, cols],
                                           PS[:, 6 + half, 0:4 * P].rearrange("p (h d) -> p h d", d=P), ACT.Relu
                                           ).then_inc(s_xm, 1)
                        if final and hd == 7 and not (isinstance(t, int) and t == 0):
                            act.wait_ge(s_z, t)
                            one = slice(t - 1, t) if isinstance(t, int) else bass.ds(t - 1, 1)
                            act.activation(zt[:], zt[:], ACT.Exp, accum_out=sq[:, one]).then_inc(s_ze, 1)

                    act.wait_ge(s_mt, 1)
                    act.sem_inc(s_xm, 2)
                    units(act, step, 8)
                    if final:
                        act.wait_ge(s_ze, NT)
                        act.activation(ve[:], sq[:], ACT.Ln).then_inc(s_ln, 1)

                @block.tensor
                def _(pe):
                    def turn(t, hd):
                        n = t * HEADS + hd
                        pe.wait_ge(s_exp, n + 1)
                        wait(pe, s_pt, n - 1)
                        for s in range(NT):
                            mm = pe.transpose(PS[:, 2 * (hd % 2) + s // 4, (s % 4) * P:(s % 4 + 1) * P],
                                              am[:, hd % 4, s * P:(s + 1) * P], ident[:])
                        mm.then_inc(s_T, 1)

                    def gather(t, hd):
                        n = t * HEADS + hd
                        pe.wait_ge(s_pt, n + 1)
                        wait(pe, s_ev, n - 1)
                        for s in range(NT):
                            mm = pe.matmul(PS[:, 4 + hd % 2, 0:CH + 1], PTr[:, hd % 2, s, :], h[:, s, hd, :],
                                           start=(s == 0), stop=(s == NT - 1))
                        mm.then_inc(s_O, 1)

                    def transposed(t, half):
                        pe.wait_ge(s_ob, 2 * t + half + 1)
                        pe.wait_ge(s_xm, 2 * t + 1 + half)
                        for k in range(4):
                            mm = pe.transpose(PS[:, 6 + half, k * P:(k + 1) * P], o[half][:, k, :], ident[:])
                        mm.then_inc(s_xt, 1)

                    def step(t, hd):
                        if not done(t):
                            turn(t, hd)
                        if (u := back(t, hd, 2)) and not (done(t) and hd >= 2):
                            gather(*u)
                        if not final and not (isinstance(t, int) and t == 0):
                            if hd == 2:
                                transposed(t - 1, 0)
                            if hd == 6:
                                transposed(t - 1, 1)

                    pe.sem_inc(s_xt, 2)
                    units(pe, step, 7)

                @block.gpsimd
                def _(pool):
                    pool.wait_ge(s_bias, 16)

                    def step(t, hd):
                        if not done(t):
                            pool.wait_ge(s_pre, t * HEADS + hd + 1)
                            pool.tensor_tensor(am[:, hd % 4, :], am[:, hd % 4, :], r4[:, hd % 2, :], ALU.add
                                               ).then_inc(s_sum, 1)
                        if final or hd not in (0, 4) or (isinstance(t, int) and t == 0):
                            return
                        half = hd // 4
                        pool.wait_ge(s_ev, HEADS * (t - 1) + 4 * (half + 1))
                        oh = o[half][:].rearrange("p h c -> p (h c)")
                        pool.tensor_tensor(oh, oh, bias[:, half * 4 * CH:(half + 1) * 4 * CH], ALU.add).then_inc(s_ob, 1)

                    units(pool, step, 5)

        phase()
        layernorm("ln2", x, xln, xT, keep=False)
        h1 = place("h1", [P, NT, HEADS, CH1 + 1], F32, 112 * KIB)
        W1t = place("W1t", [P, KD, F1], F32, 145 * KIB)
        v1 = place("v1", [P, KD, 2 * HEADS], F32, 206 * KIB)
        phase()
        project("p1", KD, CH1, xT, W1t, ins["L1_gnn_W1"], ins["L1_gnn_att_src1"], ins["L1_gnn_att_dst1"], h1, v1,
                a_dram[0])
        phase()
        attend("a1", CH1, h1, ins["L1_gnn_b1"], False)
        h2 = place("h2", [P, NT, HEADS, CH2 + 1], F32, 112 * KIB)
        W2t = place("W2t", [P, KF, HEADS * CH2], F32, 129 * KIB)
        v2 = place("v2", [P, KF, 2 * HEADS], F32, 206 * KIB)
        phase()
        project("p2", KF, CH2, x2T, W2t, ins["L1_gnn_W2"], ins["L1_gnn_att_src2"], ins["L1_gnn_att_dst2"], h2, v2,
                a_dram[1])
        phase()
        attend("a2", CH2, h2, ins["L1_gnn_b2"], True)

        xln3 = place("xln3", [P, NT, D], F32, 48 * KIB)
        xT3 = place("xT3", [P, KD, N], F32, 64 * KIB)
        w1a = place("w1a", [P, NX1, KD, H], F32, 16 * KIB)
        w2a = place("w2a", [P, NX1, HC, D], F32, 161 * KIB)
        b1r = place("b1r", [1, NX1 * H], F32, 193 * KIB)
        r1 = router_buffers("r1", NX1, 1, NB1, True, 112 * KIB)
        assert r1["end"] <= 130 * KIB
        s_wa = lasting("w_all")
        phase()
        layernorm("ln3", x, xln3, xT3, keep=True)
        phase()
        routing("rt1", NX1, 1, ins["L1_ffn_Wr"], ins["L1_ffn_br"], ins["L1_ffn_b2"], True, NB1, slot1_dram,
                xT3, r1)
        zg = place("zg", [P, 4, D], F32, 130 * KIB)
        zgT = place("zgT", [P, 2, KD, P], F32, 138 * KIB)
        zh = place("zh", [P, 2, H], F32, 142 * KIB)
        zhT = place("zhT", [P, 2, HC, P], F32, 144 * KIB)
        zo = place("zo", [P, 4, D], F32, 146 * KIB)
        phase()
        s_zg = [sem(f"z_g{j}") for j in range(4)]
        s_zs = [sem(f"z_s{j}") for j in range(4)]
        s_t, s_tm, s_h, s_hm, s_u, s_um, s_y, s_ym = (
            sem("z_" + k) for k in ("t", "tm", "h", "hm", "u", "um", "y", "ym"))
        s_gi = sem("z_gi")
        with nc.Block() as block:
            @block.sync
            def _(sp):
                sp.dma_start(w1a[:].rearrange("p e k h -> p (e k) h"),
                             ins["L1_ffn_W1"].rearrange("e (k p) h -> p (e k) h", p=P)).then_inc(s_wa, 16)
                sp.dma_start(w2a[:].rearrange("p e k h -> p (e k) h"),
                             ins["L1_ffn_W2"].rearrange("e (k p) h -> p (e k) h", p=P)).then_inc(s_wa, 16)
                sp.dma_start(b1r[:], ins["L1_ffn_b1"].rearrange("(o e) h -> o (e h)", o=1)).then_inc(s_wa, 16)

            @block.gpsimd
            def _(pool):
                pool.memset(zg[:], 0.0).then_inc(s_gi, 1)
                pool.wait_ge(s_gi, 1)

                def store(n):
                    pool.wait_ge(s_ym, n + 1)
                    pool.indirect_dma_start(z_dram, bass.IndirectOffsetOnAxis(r1["lst"][:, n:n + 1], 0),
                                            zo[:, n % 4, :], None, bounds_check=N - 1, oob_is_err=False
                                            ).then_inc(s_zs[n % 4], 16)

                for n in range(NB1):
                    if n >= 4:
                        pool.wait_ge(s_t, n - 3)
                    pool.indirect_dma_start(zg[:, n % 4, :], None, xrow_dram,
                                            bass.IndirectOffsetOnAxis(r1["lst"][:, n:n + 1], 0), bounds_check=N - 1,
                                            oob_is_err=False).then_inc(s_zg[n % 4], 16)
                    if n >= 3:
                        store(n - 3)
                for n in range(NB1 - 3, NB1):
                    store(n)
                for j in range(4):
                    pool.wait_ge(s_zs[j], 16 * len(range(j, NB1, 4)))

            @block.tensor
            def _(pe):
                def turn(n):
                    pe.wait_ge(s_zg[n % 4], 16 * (n // 4 + 1))
                    wait(pe, s_tm, n - 1)
                    for k in range(KD):
                        mm = pe.transpose(PS[:, n % 2, k * P:(k + 1) * P], zg[:, n % 4, k * P:(k + 1) * P], ident[:])
                    mm.then_inc(s_t, 1)

                def hidden(n, e):
                    pe.wait_ge(s_tm, n + 1)
                    wait(pe, s_hm, n - 1)
                    b = PS[:, 2 + n % 2, 0:H]
                    pe.matmul(b, ones1[:], b1r[0:1, bass.ds(e * H, H)], start=True, stop=False)
                    for k in range(KD):
                        mm = pe.matmul(b, zgT[:, n % 2, k, :],
                                       w1a[:, bass.ds(e, 1), k, :].rearrange("p o h -> p (o h)"), start=False,
                                       stop=(k == KD - 1))
                    mm.then_inc(s_h, 1)

                def hturn(n):
                    pe.wait_ge(s_hm, n + 1)
                    wait(pe, s_um, n - 1)
                    for c in range(HC):
                        mm = pe.transpose(PS[:, 4 + n % 2, c * P:(c + 1) * P], zh[:, n % 2, c * P:(c + 1) * P],
                                          ident[:])
                    mm.then_inc(s_u, 1)

                def output(n, e):
                    pe.wait_ge(s_um, n + 1)
                    wait(pe, s_ym, n - 1)
                    for c in range(HC):
                        mm = pe.matmul(PS[:, 6 + n % 2, :], zhT[:, n % 2, c, :],
                                       w2a[:, bass.ds(e, 1), c, :].rearrange("p o h -> p (o h)"), start=(c == 0),
                                       stop=(c == HC - 1))
                    mm.then_inc(s_y, 1)

                turn(0)
                pe.wait_ge(s_wa, 48)
                was = None
                for n in range(NB1):
                    if n + 1 < NB1:
                        turn(n + 1)
                    e = pe.value_load(r1["owni"][0:1, n:n + 1], min_val=0, max_val=NX1 - 1)
                    hidden(n, e)
                    if n:
                        output(n - 1, was)
                    hturn(n)
                    was = e
                output(NB1 - 1, was)

            @block.scalar
            def _(act):
                for n in range(NB1):
                    act.wait_ge(s_h, n + 1)
                    wait(act, s_u, n - 1)
                    act.activation(zh[:, n % 2, :], PS[:, 2 + n % 2, 0:H], ACT.Relu).then_inc(s_hm, 1)
                    act.wait_ge(s_u, n + 1)
                    wait(act, s_y, n - 1)
                    act.copy(zhT[:, n % 2, :, :].rearrange("p c n -> p (c n)"), PS[:, 4 + n % 2, 0:H]
                             ).then_inc(s_um, 1)

            @block.vector
            def _(dve):
                for n in range(NB1 + 1):
                    if n < NB1:
                        dve.wait_ge(s_t, n + 1)
                        wait(dve, s_h, n - 1)
                        dve.tensor_copy(zgT[:, n % 2, :, :].rearrange("p k n -> p (k n)"), PS[:, n % 2, :]
                                        ).then_inc(s_tm, 1)
                    if n:
                        m = n - 1
                        dve.wait_ge(s_y, m + 1)
                        wait(dve, s_zs[m % 4], 16 * (m // 4))
                        dve.tensor_copy(zo[:, m % 4, :], PS[:, 6 + m % 2, :]).then_inc(s_ym, 1)

        zb = place("zb", [P, NT, D], F32, 130 * KIB)
        phase()
        s_zb, s_bias, s_sum, s_add, s_out = sem("f_zb"), sem("f_bias"), sem("f_sum"), sem("f_add"), sem("f_out")
        with nc.Block() as block:
            @block.sync
            def _(sp):
                sp.dma_start(zb[:], z_dram.rearrange("(t p) d -> p t d", p=P)).then_inc(s_zb, 16)
                sp.wait_ge(s_add, NT)
                sp.dma_start(out.rearrange("(t p) d -> p t d", p=P), x[:]).then_inc(s_out, 16)
                sp.wait_ge(s_out, 16)

            @block.tensor
            def _(pe):
                for t in range(NT):
                    pe.matmul(PS[:, t, :], r1["swT"][:, t * P:(t + 1) * P], r1["b2s"][:], start=True, stop=True
                              ).then_inc(s_bias, 1)

            @block.vector
            def _(dve):
                dve.wait_ge(s_zb, 16)
                for t in range(NT):
                    dve.wait_ge(s_bias, t + 1)
                    dve.tensor_tensor(zb[:, t, :], zb[:, t, :], PS[:, t, :], ALU.add).then_inc(s_sum, 1)
                    dve.wait_ge(s_sum, t + 1)
                    dve.scalar_tensor_tensor(x[:, t, :], zb[:, t, :], r1["gate"][:, t:t + 1], x[:, t, :],
                                             ALU.mult, ALU.add).then_inc(s_add, 1)



_NAMES = ["x", "src", "dst", "L0_gnn_W", "L0_gnn_b", "L0_gnn_diffusion_weights", "L0_ffn_Wg", "L0_ffn_bg",
          "L0_ffn_W1", "L0_ffn_b1", "L0_ffn_W2", "L0_ffn_b2", "L0_ffn_gamma", "L0_ffn_beta", "L1_gnn_W1",
          "L1_gnn_att_src1", "L1_gnn_att_dst1", "L1_gnn_b1", "L1_gnn_W2", "L1_gnn_att_src2", "L1_gnn_att_dst2",
          "L1_gnn_b2", "L1_ffn_Wr", "L1_ffn_br", "L1_ffn_W1", "L1_ffn_b1", "L1_ffn_W2", "L1_ffn_b2"]


def kernel(**inputs):
    import numpy as np
    import concourse.bacc as bacc
    from concourse.bass_utils import run_bass_kernel_spmd

    nc = bacc.Bacc("TRN2", target_bir_lowering=False, num_devices=1)
    arrays, aps = {}, {}
    for name in _NAMES:
        a = np.ascontiguousarray(inputs[name])
        arrays["in_" + name] = a
        aps[name] = nc.dram_tensor("in_" + name, a.shape, mybir.dt.from_np(a.dtype), kind="ExternalInput").ap()
    out = nc.dram_tensor("out_0", inputs["x"].shape, F32, kind="ExternalOutput").ap()
    build(nc, aps, out)
    r = run_bass_kernel_spmd(nc, [arrays], core_ids=[0])
    return r.results[0]["out_0"]
```

```python
from contextlib import ExitStack

import concourse.bass as bass
from concourse import mybir

ALU = mybir.AluOpType
ACT = mybir.ActivationFunctionType
F32 = mybir.dt.float32
F32R = mybir.dt.float32r
BF16 = mybir.dt.bfloat16
F16 = mybir.dt.float16
I32 = mybir.dt.int32
U32 = mybir.dt.uint32
X = mybir.AxisListType.X
RMAX = bass.bass_isa.ReduceOp.max

P = 128
KIB = 1024
NEG = -1.0e30
LN_EPS = 1e-5
NEG_SLOPE = 0.2


def build(nc, ins, out):
    x_d, src_d, dst_d = ins["x"], ins["src"], ins["dst"]
    N, D = x_d.shape
    E = src_d.shape[0]
    NT = N // P
    KD = D // P
    STEPS = ins["L0_gnn_diffusion_weights"].shape[0] - 1
    NX0, H = ins["L0_ffn_W1"].shape[0], ins["L0_ffn_W1"].shape[2]
    NX1 = ins["L1_ffn_W1"].shape[0]
    HC = H // P
    TOPK = 2
    HEADS, CH1 = ins["L1_gnn_att_src1"].shape
    CH2 = ins["L1_gnn_att_src2"].shape[1]
    F1 = HEADS * CH1
    KF = F1 // P
    EC = 4
    EP = EC * P
    EQ = E // EP
    assert E % EP == 0 and EQ <= P and N == 8 * P

    ctx = ExitStack()
    with ctx:
        used = []

        def sem(name):
            used.append(nc.alloc_semaphore(name))
            return used[-1]

        def lasting(name):
            return nc.alloc_semaphore(name)

        def recycle():
            nc.clear_and_free_semaphores(list(used))
            nc.all_engine_barrier()
            used.clear()

        def place(name, shape, dt, at):
            return nc.alloc_sbuf_tensor_at(name, shape, dt, offset=BASE + at)

        ARENA = 207 * KIB + 512
        BASE = (nc.sbuf_base + 31) // 32 * 32
        ctx.enter_context(nc.sbuf_tensor("arena", [P, ARENA // 4], F32))
        PS = ctx.enter_context(nc.psum_tensor("PS", [P, 8, 512], F32))

        x = place("x_res", [P, NT, D], F32, 0)
        xln = place("xln", [P, NT, D], F32, 16 * KIB)
        xT = place("xT", [P, KD, N], F32, 32 * KIB)
        CT = place("CT", [P, NT, N], F32, 48 * KIB)
        mask = place("mask", [P, NT, N], BF16, 80 * KIB)
        iota = place("iota", [P, N], F16, 96 * KIB)
        ident = place("ident", [P, P], F32, 98 * KIB)
        onesb = place("onesb", [P, P], BF16, 98 * KIB + 512)
        before = place("before", [P, P], BF16, 98 * KIB + 768)
        zerob = place("zerob", [P, 512], BF16, 99 * KIB)
        iotaf = place("iotaf", [P, NX0], F32, 100 * KIB)
        ones1 = place("ones1", [1, P], F32, 100 * KIB + 256)
        st = place("st", [P, NT, 6], F32, 101 * KIB)
        mv = place("mv", [P, NT, 2], F32, 101 * KIB + 256)
        ve = place("ve", [P, NT], F32, 101 * KIB + 320)
        sq = place("sq", [P, NT], F32, 101 * KIB + 352)
        rs = place("rs", [P, NT], F32, 101 * KIB + 384)
        tq = place("tq", [P, NT], F32, 101 * KIB + 416)
        rowsum = place("rowsum", [P, NT], F32, 101 * KIB + 448)
        rinv = place("rinv", [P, NT], F32, 101 * KIB + 480)
        wdiff = place("wdiff", [P, STEPS + 1], F32, 101 * KIB + 512)
        nmt = place("nmt", [P, NT], F32, 101 * KIB + 544)

        xs_dram = [nc.dram_tensor(f"xs{n}_scratch", (N * k + P, D), F32, kind="Internal").ap() for n, k in ((0, TOPK), (1, 1))]
        ys_dram = [nc.dram_tensor(f"ys{n}_scratch", (N * k + P, D), F32, kind="Internal").ap() for n, k in ((0, TOPK), (1, 1))]
        NB0 = NX0 + (N * TOPK) // (P + 1)
        NB1 = NX1 + (N - NX1) // P
        q_dram = [nc.dram_tensor(f"q{n}_scratch", (HEADS, N), F32, kind="Internal").ap() for n in (1, 2)]
        a_dram = [nc.dram_tensor(f"a{n}_scratch", (2 * HEADS, N), F32, kind="Internal").ap() for n in (1, 2)]

        def bcast(v, n):
            return v.rearrange("(o n) -> o n", o=1).to_broadcast([P, n])

        def within(value, least, most):
            return nc.s_assert_within(value, least, most,
                                      skip_runtime_bounds_check_because="it follows from the loop's bounds")

        def phase():
            if len(used) > 70:
                recycle()

        def layernorm(name, src, xln, xT, loaded=None):
            s_stat, s_sqrt, s_tiles = sem(name + "_stat"), sem(name + "_sqrt"), sem(name + "_tiles")
            s_turned, s_moved = sem(name + "_turned"), sem(name + "_moved")
            s_chain = sem(name + "_chain")
            with nc.Block() as block:
                @block.vector
                def _(dve):
                    n = [0]

                    def link(ins):
                        n[0] += 1
                        ins.then_inc(s_chain, 1)
                        dve.wait_ge(s_chain, n[0])

                    if loaded is not None:
                        dve.wait_ge(loaded, 16)
                    for t in range(NT):
                        last = dve.bn_stats(st[:, t, :], src[:, t, :])
                    link(last)
                    for t in range(NT):
                        last = dve.bn_aggr(mv[:, t, :], st[:, t, :])
                    link(last)
                    dve.tensor_scalar(ve[:], mv[:, :, 1], LN_EPS, None, ALU.add).then_inc(s_stat, 1)
                    dve.wait_ge(s_sqrt, 1)
                    link(dve.reciprocal(tq[:], sq[:]))
                    link(dve.tensor_tensor(tq[:], tq[:], ve[:], ALU.mult))
                    link(dve.tensor_tensor(tq[:], tq[:], sq[:], ALU.add))
                    link(dve.tensor_scalar(tq[:], tq[:], 0.5, None, ALU.mult))
                    link(dve.reciprocal(rs[:], tq[:]))
                    for t in range(NT):
                        dve.tensor_scalar(xln[:, t, :], src[:, t, :], mv[:, t, 0:1], rs[:, t:t + 1],
                                          ALU.subtract, ALU.mult).then_inc(s_tiles, 1)

                @block.scalar
                def _(act):
                    act.wait_ge(s_stat, 1)
                    act.activation(sq[:], ve[:], ACT.Sqrt).then_inc(s_sqrt, 1)
                    for t in range(NT):
                        act.wait_ge(s_turned, t + 1)
                        act.copy(xT[:, :, t * P:(t + 1) * P],
                                 PS[:, t % 2, :].rearrange("p (k n) -> p k n", k=KD)).then_inc(s_moved, 1)

                @block.tensor
                def _(pe):
                    for t in range(NT):
                        pe.wait_ge(s_tiles, t + 1)
                        if t >= 2:
                            pe.wait_ge(s_moved, t - 1)
                        for k in range(KD):
                            last = pe.transpose(PS[:, t % 2, k * P:(k + 1) * P], xln[:, t, k * P:(k + 1) * P],
                                                ident[:])
                        last.then_inc(s_turned, 1)

        srcq = place("srcq", [EQ, EP], I32, 112 * KIB)
        dstq = place("dstq", [EQ, EP], I32, 114 * KIB)
        srcf = place("srcf", [EQ, EP], F32, 116 * KIB)
        dstf = place("dstf", [EQ, EP], F32, 118 * KIB)
        tili = place("tili", [EQ, EP], I32, 120 * KIB)
        tilf = place("tilf", [EQ, EP], F32, 122 * KIB)
        C = place("C", [P, NT, N], F32, 112 * KIB)
        adj = place("adj", [P, NT, N], F32R, 144 * KIB)
        oh_src = place("oh_src", [P, 2, EC, N], BF16, 176 * KIB)
        oh_dst = place("oh_dst", [P, 2, EC, P], BF16, 202 * KIB)
        eT = place("eT", [P, 2, EC, EQ], F32, 204 * KIB)
        W0 = place("W0", [P, KD, D], F32, 192 * KIB)
        b0 = place("b0", [P, D], F32, 200 * KIB)
        reach = place("reach", [EQ, 2 * NT], F32, 206 * KIB)
        reachm = place("reachm", [EQ, 2 * NT], F32, 206 * KIB + 64)
        tmm = place("tmm", [EQ, 2], F32, 206 * KIB + 128)
        qcol = place("qcol", [EQ, 2], F32, 206 * KIB + 160)
        act8 = place("act8", [EQ, 2, NT], F32, 206 * KIB + 192)
        rows = place("rows", [1, 6, NT], F32, 206 * KIB + 256)
        rowi = place("rowi", [1, 3, NT], I32, 206 * KIB + 512)
        both = place("both", [P, 2, N], F32, 176 * KIB)

        s_in_x, s_in_e, s_in_w = lasting("in_x"), lasting("in_edges"), lasting("in_w")

        phase()
        s_const, s_eflt, s_eturn, s_eT = sem("const"), sem("edges_float"), sem("edges_turned"), sem("eT_ready")
        s_reach, s_reachm, s_range = sem("reach"), sem("reach_max"), sem("range_ready")
        s_free, s_hot, s_tile, s_C = sem("onehot_free"), sem("onehot_ready"), sem("C_summed"), sem("C_moved")
        s_ctt, s_ctm, s_both, s_adj = sem("CT_turned"), sem("CT_moved"), sem("both_ready"), sem("adj_moved")
        s_chain, s_chp = sem("prep_chain"), sem("prep_chain_pool")
        with nc.Block() as block:
            @block.sync
            def _(sp):
                sp.dma_start(dstq[:], dst_d.rearrange("(q e) -> q e", e=EP)).then_inc(s_in_e, 16)
                sp.dma_start(srcq[:], src_d.rearrange("(q e) -> q e", e=EP)).then_inc(s_in_e, 16)
                sp.dma_start(x[:], x_d.rearrange("(t p) d -> p t d", p=P)).then_inc(s_in_x, 16)
                sp.dma_start(W0[:], ins["L0_gnn_W"].rearrange("(k p) n -> p k n", p=P)).then_inc(s_in_w, 16)
                sp.dma_start(b0[:], bcast(ins["L0_gnn_b"], D)).then_inc(s_in_w, 16)
                sp.dma_start(wdiff[:], bcast(ins["L0_gnn_diffusion_weights"], STEPS + 1)).then_inc(s_in_w, 16)

            @block.gpsimd
            def _(pool):
                n = [0]

                def link(ins):
                    n[0] += 1
                    ins.then_inc(s_chp, 1)
                    pool.wait_ge(s_chp, n[0])

                pool.iota(iota[:], [[1, N]], 0, 0, allow_small_or_imprecise_dtypes=True)
                pool.iota(qcol[:, 0:1], [[0, 1]], 1, 1, allow_small_or_imprecise_dtypes=True)
                pool.iota(qcol[:, 1:2], [[0, 1]], EQ, -1, allow_small_or_imprecise_dtypes=True)
                pool.iota(iotaf[:], [[1, NX0]], 0, 0, allow_small_or_imprecise_dtypes=True)
                pool.memset(onesb[:], 1.0)
                pool.memset(ones1[:], 1.0)
                pool.memset(zerob[:], 0.0)
                pool.memset(ident[:], 0.0)
                link(pool.memset(before[:], 1.0))
                pool.affine_select(before[:], before[:], [[1, P]], ALU.is_gt, 0.0, base=0, channel_multiplier=-1)
                pool.affine_select(ident[:], ident[:], [[1, P]], ALU.not_equal, 1.0, base=0,
                                   channel_multiplier=-1).then_inc(s_const, 1)
                pool.wait_ge(s_reach, 1)
                pool.partition_all_reduce(reachm[:], reach[:], EQ, RMAX).then_inc(s_reachm, 1)
                for t in range(NT):
                    own = slice(t * P, (t + 1) * P)
                    pool.wait_ge(s_C, t + 1)
                    link(pool.tensor_scalar(mask[:, t, :], C[:, t, :], 0.0, NEG, ALU.is_equal, ALU.mult))
                    link(pool.affine_select(mask[:, t, own], mask[:, t, own], [[1, P]], ALU.not_equal, 0.0, base=0,
                                            channel_multiplier=-1))

            @block.vector
            def _(dve):
                n = [0]

                def link(ins):
                    n[0] += 1
                    ins.then_inc(s_chain, 1)
                    dve.wait_ge(s_chain, n[0])

                dve.wait_ge(s_in_e, 32)
                dve.tensor_copy(srcf[:], srcq[:])
                dve.tensor_copy(dstf[:], dstq[:]).then_inc(s_eflt, 1)
                link(dve.tensor_scalar(tili[:], dstq[:], P.bit_length() - 1, None, ALU.logical_shift_right))
                link(dve.tensor_copy(tilf[:], tili[:]))
                dve.tensor_reduce(tmm[:, 0:1], tilf[:], X, ALU.min)
                link(dve.tensor_reduce(tmm[:, 1:2], tilf[:], X, ALU.max))
                dve.wait_ge(s_const, 1)
                dve.tensor_scalar(act8[:, 0, :], iotaf[0:EQ, 0:NT], tmm[:, 0:1], None, ALU.is_ge)
                link(dve.tensor_scalar(act8[:, 1, :], iotaf[0:EQ, 0:NT], tmm[:, 1:2], None, ALU.is_le))
                link(dve.tensor_tensor(act8[:, 0, :], act8[:, 0, :], act8[:, 1, :], ALU.mult))
                dve.tensor_scalar(reach[:, 0:NT], act8[:, 0, :], qcol[:, 0:1], None, ALU.mult)
                dve.tensor_scalar(reach[:, NT:2 * NT], act8[:, 0, :], qcol[:, 1:2], None,
                                  ALU.mult).then_inc(s_reach, 1)
                dve.wait_ge(s_eturn, 1)
                dve.tensor_copy(eT[:].rearrange("p a c q -> p (a c q)"), PS[:, 0, 0:2 * EC * EQ]).then_inc(s_eT, 1)
                dve.wait_ge(s_reachm, 1)
                LO, HI, CNT, END, BEG, DEL = (rows[:, k, :] for k in range(6))
                link(dve.tensor_scalar(LO, reachm[0:1, NT:2 * NT], -1.0, float(EQ), ALU.mult, ALU.add))
                link(dve.tensor_scalar(LO, LO, float(EQ - 1), None, ALU.min))
                link(dve.tensor_scalar(HI, LO, 1.0, None, ALU.add))
                link(dve.tensor_tensor(HI, HI, reachm[0:1, 0:NT], ALU.max))
                link(dve.tensor_tensor(CNT, HI, LO, ALU.subtract))
                link(dve.tensor_tensor_scan(END, CNT, CNT, 0.0, ALU.add, ALU.bypass))
                link(dve.tensor_tensor(BEG, END, CNT, ALU.subtract))
                link(dve.tensor_tensor(DEL, LO, BEG, ALU.subtract))
                dve.tensor_copy(rowi[:, 0, :], BEG)
                dve.tensor_copy(rowi[:, 1, :], END)
                dve.tensor_copy(rowi[:, 2, :], DEL).then_inc(s_range, 1)
                dve.wait_ge(s_range, 1)
                for t in range(NT):
                    first = dve.value_load(rowi[0:1, 0, t:t + 1], min_val=0, max_val=NT * EQ)
                    last = dve.value_load(rowi[0:1, 1, t:t + 1], min_val=1, max_val=NT * EQ)
                    shift = dve.value_load(rowi[0:1, 2, t:t + 1], min_val=-NT * EQ, max_val=EQ)
                    with dve.Fori(first, last) as u:
                        q = within(dve.snap(u + shift), 0, EQ - 1)
                        slot = within(dve.snap(u % 2), 0, 1)
                        dve.wait_ge(s_free, u + 1)
                        for c in range(EC):
                            dve.tensor_scalar(oh_src[:, bass.ds(slot, 1), c, :], iota[:],
                                              eT[:, 0, c, bass.ds(q, 1)], None, ALU.is_equal)
                            ins_ = dve.tensor_scalar(oh_dst[:, bass.ds(slot, 1), c, :],
                                                     iota[:, t * P:(t + 1) * P],
                                                     eT[:, 1, c, bass.ds(q, 1)], None, ALU.is_equal)
                        ins_.then_inc(s_hot, 1)
                for i in range(NT):
                    own = slice(i * P, (i + 1) * P)
                    dve.wait_ge(s_ctt, i + 1)
                    if i >= 2:
                        dve.wait_ge(s_adj, i - 1)
                    if i == 0:
                        dve.wait_ge(s_C, NT)
                    link(dve.tensor_tensor(both[:, i % 2, :], C[:, i, :],
                                           PS[:, 4 + 2 * (i % 2):6 + 2 * (i % 2), :].rearrange("p a n -> p (a n)"),
                                           ALU.add))
                    link(dve.tensor_scalar(both[:, i % 2, :], both[:, i % 2, :], 1.0, None, ALU.min, ALU.add,
                                           accum_out=rowsum[:, i:i + 1]))
                    dve.tensor_tensor(both[:, i % 2, own], both[:, i % 2, own], ident[:],
                                      ALU.add).then_inc(s_both, 1)
                    dve.wait_ge(s_ctm, i + 1)
                    dve.tensor_tensor(CT[:, i, own], CT[:, i, own], ident[:], ALU.add)
                link(dve.tensor_scalar(rowsum[:], rowsum[:], 1.0, 1.0, ALU.add, ALU.max))
                link(dve.reciprocal(rinv[:], rowsum[:]))

            @block.scalar
            def _(act):
                for t in range(NT):
                    act.wait_ge(s_tile, t + 1)
                    act.copy(C[:, t, :], PS[:, 2 * (t % 2):2 * (t % 2) + 2, :].rearrange("p a n -> p (a n)")
                             ).then_inc(s_C, 1)
                for i in range(NT):
                    act.wait_ge(s_both, i + 1)
                    act.copy(CT[:, i, :], PS[:, 4 + 2 * (i % 2):6 + 2 * (i % 2), :].rearrange("p a n -> p (a n)")
                             ).then_inc(s_ctm, 1)
                    act.copy(adj[:, i, :], both[:, i % 2, :]).then_inc(s_adj, 1)

            @block.tensor
            def _(pe):
                pe.wait_ge(s_const, 1)
                pe.wait_ge(s_eflt, 1)
                for a, e in enumerate((srcf, dstf)):
                    for c in range(EC):
                        last = pe.transpose(PS[:, 0, (EC * a + c) * EQ:(EC * a + c + 1) * EQ],
                                            e[:, c * P:(c + 1) * P], ident[0:EQ, 0:EQ])
                last.then_inc(s_eturn, 1)
                pe.wait_ge(s_eT, 1)
                pe.wait_ge(s_range, 1)
                pe.sem_inc(s_free, 2)
                for t in range(NT):
                    first = pe.value_load(rowi[0:1, 0, t:t + 1], min_val=0, max_val=NT * EQ)
                    last = pe.value_load(rowi[0:1, 1, t:t + 1], min_val=1, max_val=NT * EQ)
                    if t >= 2:
                        pe.wait_ge(s_C, t - 1)
                    for h in range(2):
                        pe.matmul(PS[:, 2 * (t % 2) + h, :], onesb[:], zerob[:], start=True, stop=False)
                    with pe.Fori(first, last) as u:
                        slot = within(pe.snap(u % 2), 0, 1)
                        pe.wait_ge(s_hot, u + 1)
                        for c in range(EC):
                            for h in range(2):
                                mm = pe.matmul(PS[:, 2 * (t % 2) + h, :], oh_dst[:, bass.ds(slot, 1), c, :],
                                               oh_src[:, bass.ds(slot, 1), c, h * 512:(h + 1) * 512],
                                               start=False, stop=False)
                        mm.then_inc(s_free, 1)
                    for h in range(2):
                        mm = pe.matmul(PS[:, 2 * (t % 2) + h, :], onesb[:], zerob[:], start=False, stop=True)
                    mm.then_inc(s_tile, 1)
                pe.wait_ge(s_C, NT)
                for i in range(NT):
                    if i >= 2:
                        pe.wait_ge(s_ctm, i - 1)
                    for j in range(NT):
                        mm = pe.transpose(PS[:, 4 + 2 * (i % 2) + j // 4, (j % 4) * P:(j % 4 + 1) * P],
                                          C[:, j, i * P:(i + 1) * P], ident[:])
                    mm.then_inc(s_ctt, 1)

        phase()
        layernorm("ln0", x, xln, xT, loaded=s_in_x)
        hi = [place("hi0", [P, NT, D], F32R, 112 * KIB), place("hi1", [P, NT, D], F32R, 16 * KIB)]
        lo = [place("lo0", [P, NT, D], F32R, 128 * KIB), place("lo1", [P, NT, D], F32R, 32 * KIB)]
        acc = place("acc", [P, NT, D], F32, 176 * KIB)
        least1 = place("least1", [P, 2, N], F32, 192 * KIB)
        cur = place("cur", [P, 2, D], F32, 202 * KIB)
        phase()
        s_sum, s_cur, s_hi, s_lo, s_acc = (sem("gnn_" + k) for k in ("sum", "cur", "hi", "lo", "acc"))
        s_chain = sem("gnn_chain")
        s_one, s_ln, s_none, s_log = (sem("gnn_" + k) for k in ("one", "ln", "none", "log"))
        with nc.Block() as block:
            @block.gpsimd
            def _(pool):
                pool.wait_ge(s_cur, NT)
                for s in range(NT):
                    if s >= 2:
                        pool.wait_ge(s_log, s - 1)
                    pool.tensor_scalar(least1[:, s % 2, :], CT[:, s, :], 1.0, None, ALU.max).then_inc(s_one, 1)
                    pool.tensor_scalar(CT[:, s, :], CT[:, s, :], 0.0, NEG, ALU.is_equal, ALU.mult
                                       ).then_inc(s_none, 1)

            @block.tensor
            def _(pe):
                for i in range(STEPS + 1):
                    if i:
                        pe.wait_ge(s_lo, NT * i)
                        pe.wait_ge(s_hi, NT * i)
                    else:
                        pe.wait_ge(s_in_w, 48)
                    for t in range(NT):
                        n = i * NT + t
                        if n >= 2:
                            pe.wait_ge(s_cur, n - 1)
                        if i == 0:
                            for k in range(KD):
                                mm = pe.matmul(PS[:, n % 2, :], xT[:, k, t * P:(t + 1) * P], W0[:, k, :],
                                               start=(k == 0), stop=(k == KD - 1))
                        else:
                            for j in range(NT):
                                for part in (hi, lo):
                                    mm = pe.matmul(PS[:, n % 2, :], adj[:, j, t * P:(t + 1) * P],
                                                   part[(i + 1) % 2][:, j, :], start=(j == 0 and part is hi),
                                                   stop=(j == NT - 1 and part is lo))
                        mm.then_inc(s_sum, 1)

            @block.scalar
            def _(act):
                for i in range(STEPS + 1):
                    for t in range(NT):
                        n = i * NT + t
                        if i:
                            act.wait_ge(s_sum, n + 1)
                            if n >= 2:
                                act.wait_ge(s_acc, n - 1)
                            act.activation(cur[:, n % 2, :], PS[:, n % 2, :], ACT.Copy,
                                           scale=rinv[:, t:t + 1]).then_inc(s_cur, 1)
                        act.wait_ge(s_cur, n + 1)
                        if n >= 10 and (n - 10) % 3 == 0:
                            s = (n - 10) // 3
                            act.wait_ge(s_one, s + 1)
                            act.activation(least1[:, s % 2, :], least1[:, s % 2, :], ACT.Ln).then_inc(s_ln, 1)
                        act.copy(hi[i % 2][:, t, :], cur[:, n % 2, :]).then_inc(s_hi, 1)

            @block.vector
            def _(dve):
                n_link = [0]

                def link(ins):
                    n_link[0] += 1
                    ins.then_inc(s_chain, 1)
                    dve.wait_ge(s_chain, n_link[0])

                def logs(s):
                    dve.wait_ge(s_ln, s + 1)
                    dve.wait_ge(s_none, s + 1)
                    dve.scalar_tensor_tensor(CT[:, s, :], least1[:, s % 2, :], 1 / (1 - NEG_SLOPE), CT[:, s, :],
                                             ALU.mult, ALU.add).then_inc(s_log, 1)

                for i in range(STEPS + 1):
                    for t in range(NT):
                        n = i * NT + t
                        if n >= 11 and (n - 11) % 3 == 0:
                            logs((n - 11) // 3)
                        if i == 0:
                            dve.wait_ge(s_sum, n + 1)
                            dve.tensor_tensor(cur[:, n % 2, :], PS[:, n % 2, :], b0[:], ALU.add
                                              ).then_inc(s_cur, 1)
                            dve.wait_ge(s_cur, n + 1)
                            link(dve.tensor_scalar(acc[:, t, :], cur[:, n % 2, :], wdiff[:, 0:1], None, ALU.mult))
                        else:
                            dve.wait_ge(s_cur, n + 1)
                            link(dve.scalar_tensor_tensor(acc[:, t, :], cur[:, n % 2, :], wdiff[:, i:i + 1],
                                                          acc[:, t, :], ALU.mult, ALU.add))
                        dve.wait_ge(s_hi, n + 1)
                        dve.tensor_tensor(lo[i % 2][:, t, :], cur[:, n % 2, :], hi[i % 2][:, t, :].bitcast(F32),
                                          ALU.subtract).then_inc(s_lo, 1)
                        if i == STEPS:
                            dve.scalar_tensor_tensor(x[:, t, :], acc[:, t, :], 0.0, x[:, t, :], ALU.max, ALU.add
                                                     ).then_inc(s_acc, 1)
                        else:
                            dve.wait_ge(s_lo, n + 1)
                            dve.sem_inc(s_acc, 1)
                logs(NT - 1)

        def routing(name, X0, K, logits_w, bias_d, b2_d, flat, NB, xs, xln, xT, sb, prefetch):
            s_w, s_log, s_logm, s_exp, s_pick = (sem(f"{name}_{k}") for k in ("w", "logits", "moved", "exp", "pick"))
            s_rank, s_pos, s_jt, s_sc, s_behind = (sem(f"{name}_{k}") for k in ("rank", "pos", "jtab", "scattered", "behind"))
            s_chain, s_lead, s_gate = sem(name + "_chain"), sem(name + "_lead"), sem(name + "_gate")
            s_sw = sem(name + "_sw")
            s_tw, s_twm, s_ready = sem(name + "_tw"), sem(name + "_twm"), sem(name + "_ready")
            wg, bg, lg, top, idx = sb["wg"], sb["bg"], sb["lg"], sb["top"], sb["idx"]
            idxf, M, Mb, nm, sm, rm = sb["idxf"], sb["M"], sb["Mb"], sb["nm"], sb["sm"], sb["rm"]
            sw, swT, cnt, nb, cum, beg = sb["sw"], sb["swT"], sb["cnt"], sb["nb"], sb["cum"], sb["beg"]
            first, more, off, offo, nbi = sb["first"], sb["more"], sb["off"], sb["offo"], sb["nbi"]
            G, MG, pos, posi, offi = sb["G"], sb["MG"], sb["pos"], sb["posi"], sb["offi"]
            jtab, c0, c1, own, owni, start, starti = (
                sb[k] for k in ("jtab", "c0", "c1", "own", "owni", "start", "starti"))
            b2s = sb["b2s"]
            NO = NB if flat else NB - X0
            LOGP = P.bit_length() - 1
            with nc.Block() as block:
                @block.sync
                def _(sp):
                    sp.dma_start(wg[:], logits_w.rearrange("(k p) n -> p k n", p=P)).then_inc(s_w, 16)
                    sp.dma_start(bg[:], bcast(bias_d, X0)).then_inc(s_w, 16)
                    sp.dma_start(b2s[:], b2_d).then_inc(s_w, 16)
                    prefetch(sp)
                    sp.dma_start(xs[N * K:N * K + P, :], xln[:, 0, :]).then_inc(s_behind, 16)
                    sp.wait_ge(s_behind, 16)

                @block.gpsimd
                def _(pool):
                    pool.iota(jtab[:], [[1, NO], [0, X0]], 0, 0, allow_small_or_imprecise_dtypes=True).then_inc(s_jt, 1)
                    pool.wait_ge(s_pos, 1)
                    for t in range(NT):
                        for k in range(K):
                            pool.indirect_dma_start(xs, bass.IndirectOffsetOnAxis(posi[:, t, k:k + 1], 0),
                                                    xln[:, t, :], None).then_inc(s_sc, 16)
                    pool.wait_ge(s_sc, 16 * NT * K)

                @block.tensor
                def _(pe):
                    pe.wait_ge(s_w, 48)
                    for t in range(NT):
                        if t >= 2:
                            pe.wait_ge(s_logm, t - 1)
                        for k in range(KD):
                            mm = pe.matmul(PS[:, t % 2, 0:X0], xT[:, k, t * P:(t + 1) * P], wg[:, k, :],
                                           start=(k == 0), stop=(k == KD - 1))
                        mm.then_inc(s_log, 1)
                    pe.wait_ge(s_pick, 1)
                    for t in range(NT + 1):
                        o = PS[:, 2 + t // 8, (t % 8) * X0:(t % 8 + 1) * X0]
                        for j in range(min(t, NT)):
                            pe.matmul(o, onesb[:], Mb[:, j, :], start=(j == 0), stop=(t == NT and j == NT - 1))
                        if t < NT:
                            mm = pe.matmul(o, before[:], Mb[:, t, :], start=(t == 0), stop=True)
                    pe.matmul(PS[:, 4, 0:X0], onesb[:], zerob[:, 0:X0], start=True, stop=True).then_inc(s_rank, 1)
                    pe.wait_ge(s_sw, 1)
                    for t in range(NT):
                        mm = pe.transpose(PS[0:X0, 6 + t // 4, (t % 4) * P:(t % 4 + 1) * P], sw[:, t, :], ident[:])
                    mm.then_inc(s_tw, 1)

                @block.scalar
                def _(act):
                    if K == 1:
                        act.wait_ge(s_lead, 1)
                        act.activation(sb["gate"][:], sm[:], ACT.Exp).then_inc(s_gate, 1)
                    for t in range(NT if K > 1 else 0):
                        act.wait_ge(s_ready, t + 1)
                        act.activation(lg[:, t, :], lg[:, t, :], ACT.Exp, bias=nm[:, t:t + 1],
                                       accum_out=sm[:, t:t + 1]).then_inc(s_exp, 1)
                    act.wait_ge(s_tw, 1)
                    act.copy(swT[:], PS[0:X0, 6:8, :].rearrange("p a n -> p (a n)")).then_inc(s_twm, 1)

                @block.vector
                def _(dve):
                    n = [0]

                    def link(ins):
                        n[0] += 1
                        ins.then_inc(s_chain, 1)
                        dve.wait_ge(s_chain, n[0])

                    dve.wait_ge(s_w, 48)
                    for t in range(NT):
                        dve.wait_ge(s_log, t + 1)
                        dve.tensor_tensor(lg[:, t, :], PS[:, t % 2, 0:X0], bg[:], ALU.add).then_inc(s_logm, 1)
                        dve.wait_ge(s_logm, t + 1)
                        link(dve.tensor_reduce(nm[:, t:t + 1], lg[:, t, :], X, ALU.max))
                        if K == 1:
                            link(dve.max(top[:, t, :], lg[:, t, :]))
                            link(dve.max_index(idx[:, t, :], top[:, t, :], lg[:, t, :]))
                        dve.tensor_scalar(nm[:, t:t + 1], nm[:, t:t + 1], -1.0, None, ALU.mult).then_inc(s_ready, 1)
                    for t in range(NT):
                        if K > 1:
                            dve.wait_ge(s_exp, t + 1)
                            dve.reciprocal(rm[:, t:t + 1], sm[:, t:t + 1])
                            link(dve.max(top[:, t, :], lg[:, t, :]))
                            link(dve.max_index(idx[:, t, :], top[:, t, :], lg[:, t, :]))
                    if K == 1:
                        dve.wait_ge(s_ready, NT)
                        dve.tensor_tensor(sm[:], top[:, :, 0], nm[:], ALU.add).then_inc(s_lead, 1)
                        dve.wait_ge(s_gate, 1)
                        link(dve.reciprocal(rm[:], sb["gate"][:]))
                        link(dve.tensor_tensor(sb["gate"][:], sb["gate"][:], rm[:], ALU.mult))
                    link(dve.tensor_copy(idxf[:], idx[:, :, 0:K]))
                    last = dve.tensor_tensor(M[:].rearrange("p t k e -> p (t k) e"),
                                             iotaf[:, 0:X0].unsqueeze(1).to_broadcast([P, NT * K, X0]),
                                             idxf[:].rearrange("p t k -> p (t k)").unsqueeze(2).to_broadcast(
                                                 [P, NT * K, X0]), ALU.is_equal)
                    if K > 1:
                        link(last)
                        dve.tensor_tensor(Mb[:], M[:, :, 0, :], M[:, :, 1, :], ALU.add).then_inc(s_pick, 1)
                    else:
                        link(last)
                        dve.tensor_copy(Mb[:], M[:, :, 0, :]).then_inc(s_pick, 1)
                    dve.wait_ge(s_rank, 1)
                    link(dve.tensor_copy(cnt[:], PS[:, 3, 0:X0]))
                    def summed(dst, src):
                        link(dve.tensor_tensor_scan(dst[:], src[:], src[:], 0.0, ALU.add, ALU.bypass))

                    def over_tokens(v):
                        return v[:].unsqueeze(1).to_broadcast([P, NT, X0])

                    rank = PS[:, 2, 0:NT * X0].rearrange("p (t e) -> p t e", e=X0)
                    if flat:
                        summed(off, cnt)
                        link(dve.tensor_tensor(off[:], off[:], cnt[:], ALU.subtract))
                        link(dve.tensor_tensor(G[:], rank, over_tokens(off), ALU.add))
                    else:
                        link(dve.tensor_scalar(first[:], cnt[:], float(P), None, ALU.min))
                        link(dve.tensor_tensor(more[:], cnt[:], first[:], ALU.subtract))
                        summed(off, first)
                        summed(offo, more)
                        link(dve.tensor_tensor(offo[:], offo[:], more[:], ALU.subtract))
                        link(dve.tensor_scalar(offo[:], offo[:], off[:, X0 - 1:X0], None, ALU.add))
                        link(dve.tensor_tensor(off[:], off[:], first[:], ALU.subtract))
                        link(dve.scalar_tensor_tensor(beg[:], offo[:], float(-P), off[:], ALU.add, ALU.subtract))
                        link(dve.scalar_tensor_tensor(G[:], rank, float(P), over_tokens(beg), ALU.is_ge, ALU.mult))
                        link(dve.tensor_tensor(G[:], G[:], rank, ALU.add))
                        link(dve.tensor_tensor(G[:], G[:], over_tokens(off), ALU.add))
                    link(dve.tensor_tensor(MG[:], M[:], G[:].unsqueeze(2).to_broadcast([P, NT, K, X0]), ALU.mult))
                    link(dve.tensor_reduce(pos[:].rearrange("p t k -> p (t k)"), MG[:].rearrange(
                        "p t k e -> p (t k) e"), X, ALU.add))
                    dve.tensor_copy(posi[:], pos[:]).then_inc(s_pos, 1)
                    if K > 1:
                        for t in range(NT):
                            last = dve.tensor_scalar(top[:, t, :], top[:, t, :], rm[:, t:t + 1], None, ALU.mult)
                        link(last)
                        for t in range(NT):
                            last = dve.tensor_scalar(sw[:, t, :], M[:, t, 0, :], top[:, t, 0:1], None, ALU.mult)
                        link(last)
                        for t in range(NT):
                            last = dve.scalar_tensor_tensor(sw[:, t, :], M[:, t, 1, :], top[:, t, 1:2], sw[:, t, :],
                                                            ALU.mult, ALU.add)
                        last.then_inc(s_sw, 1)
                    else:
                        dve.tensor_copy(sw[:], M[:, :, 0, :]).then_inc(s_sw, 1)
                    link(dve.tensor_copy(offi[:], off[:]))
                    if not flat:
                        link(dve.tensor_copy(sb["firsti"][:], first[:]))
                    rows = cnt if flat else more
                    link(dve.tensor_scalar(nb[:], rows[:], float(P - 1), None, ALU.add))
                    link(dve.tensor_copy(nbi[:], nb[:]))
                    link(dve.tensor_scalar(nbi[:], nbi[:], LOGP, None, ALU.logical_shift_right))
                    link(dve.tensor_copy(nb[:], nbi[:]))
                    summed(cum, nb)
                    link(dve.tensor_tensor(beg[:], cum[:], nb[:], ALU.subtract))
                    link(dve.scalar_tensor_tensor(nb[:], beg[:], float(-P), (off if flat else offo)[:], ALU.mult,
                                                  ALU.add))
                    link(dve.tensor_scalar(nb[:], nb[:], float(-N * K), None, ALU.add))
                    dve.wait_ge(s_jt, 1)

                    def over_blocks(v):
                        return v[0:1, :].unsqueeze(1).to_broadcast([1, NO, X0])

                    link(dve.tensor_tensor(c1[:], jtab[:], over_blocks(cum), ALU.is_ge))
                    link(dve.tensor_reduce(own[:, 0:NO], c1[:], X, ALU.add))
                    link(dve.tensor_scalar(own[:, 0:NO], own[:, 0:NO], float(X0 - 1), None, ALU.min))
                    link(dve.tensor_copy(own[:, NO:NO + 1], cum[0:1, X0 - 1:X0]))
                    link(dve.tensor_copy(owni[:], own[:]))
                    link(dve.tensor_tensor(c0[:], jtab[:], over_blocks(beg), ALU.is_ge))
                    link(dve.tensor_tensor(c0[:], c0[:], c1[:], ALU.subtract))
                    link(dve.scalar_tensor_tensor(c1[:], jtab[:], float(P), over_blocks(nb), ALU.mult, ALU.add))
                    link(dve.tensor_tensor(c0[:], c0[:], c1[:], ALU.mult))
                    link(dve.tensor_reduce(start[:], c0[:], X, ALU.add))
                    link(dve.tensor_scalar(start[:], start[:], float(N * K), None, ALU.add))
                    link(dve.tensor_copy(starti[:], start[:]))

        def router_buffers(tag, X0, K, NB, flat, at, scratch=None):
            NO = NB if flat else NB - X0
            names = dict(
                wg=([P, KD, X0], F32), bg=([P, X0], F32), lg=([P, NT, X0], F32), top=([P, NT, 8], F32),
                idx=([P, NT, 8], U32), idxf=([P, NT, K], F32), M=([P, NT, K, X0], F32), Mb=([P, NT, X0], BF16),
                nm=([P, NT], F32), sm=([P, NT], F32), rm=([P, NT], F32), sw=([P, NT, X0], F32),
                swT=([X0, N], F32), cnt=([P, X0], F32), nb=([P, X0], F32), cum=([P, X0], F32),
                beg=([P, X0], F32), first=([P, X0], F32), more=([P, X0], F32), off=([P, X0], F32),
                offo=([P, X0], F32), nbi=([P, X0], I32), pos=([P, NT, K], F32), posi=([P, NT, K], I32),
                offi=([P, X0], I32), firsti=([P, X0], I32), own=([1, NO + 1], F32), owni=([1, NO + 1], I32), start=([1, NO], F32),
                starti=([1, NO], I32), b2s=([X0, D], F32), gate=([P, NT], F32))
            passing = dict(G=([P, NT, X0], F32), MG=([P, NT, K, X0], F32), jtab=([1, NO, X0], F32),
                           c0=([1, NO, X0], F32), c1=([1, NO, X0], F32))
            made = {}
            for group in (names, passing):
                if group is passing:
                    made["end"] = at
                    at = at if scratch is None else scratch
                for k, (shape, dt) in group.items():
                    size = 2 if dt == BF16 else 4
                    for s in shape[1:]:
                        size *= s
                    made[k] = place(f"{tag}_{k}", shape, dt, at)
                    at += (size + 31) // 32 * 32
            if scratch is None:
                made["end"] = at
            return made

        r0 = router_buffers("r0", NX0, TOPK, NB0, False, 176 * KIB, 144 * KIB)
        assert r0["end"] <= 199 * KIB + 512, r0["end"] / 1024
        w1r = place("w1r", [P, 4, KD, H], F32, 112 * KIB)
        w2r = place("w2r", [P, 4, HC, D], F32, 128 * KIB)
        s_w0, s_w1 = ([lasting(f"x{n}_w{j}") for j in range(4)] for n in (0, 1))

        def load_weights(sp, W1_d, W2_d, one, j, s_w):
            sp.dma_start(w1r[:, j, :, :], W1_d[one].rearrange("o (k p) h -> p (o k) h", p=P)).then_inc(s_w[j], 16)
            sp.dma_start(w2r[:, j, :, :], W2_d[one].rearrange("o (k p) h -> p (o k) h", p=P)).then_inc(s_w[j], 16)

        def first_experts(sp):
            for e in range(4):
                load_weights(sp, ins["L0_ffn_W1"], ins["L0_ffn_W2"], slice(e, e + 1), e, s_w0)

        phase()
        layernorm("ln1", x, xln, xT)
        phase()
        routing("rt0", NX0, TOPK, ins["L0_ffn_Wg"], ins["L0_ffn_bg"], ins["L0_ffn_b2"], False, NB0,
                xs_dram[0], xln, xT, r0, first_experts)

        xg = place("xg", [P, 4, D], F32, 144 * KIB)
        xgT = place("xgT", [P, 2, KD, P], F32, 152 * KIB)
        hT = place("hT", [P, 2, HC, P], F32, 156 * KIB)
        yo = place("yo", [P, 4, D], F32, 158 * KIB)
        b1T = place("b1T", [P, HC, NX0], F32, 166 * KIB)
        b1s = place("b1s", [NX0, H], F32, 167 * KIB)
        owni = r0["owni"]
        offi, starti = r0["offi"], r0["starti"]

        def first_row(eng, table, n, rows):
            return eng.value_load(table[0:1, n:n + 1] if isinstance(n, int) else table[0:1, bass.ds(n, 1)],
                                  min_val=0, max_val=rows)

        def wait(eng, s, v):
            if not isinstance(v, int) or v > 0:
                eng.wait_ge(s, v)

        def loop(eng, body):
            for j in range(4):
                body(j, 0, j, False)
            with eng.Fori(1, NX0 // 4 - 1) as g:
                for j in range(4):
                    body(eng.snap(g * 4 + j), g, j, False)
            for j in range(4):
                body(NX0 - 4 + j, NX0 // 4 - 1, j, j == 3)

        v1 = place("v1", [P, KD, 2 * HEADS], F32, 96 * KIB)
        v2 = place("v2", [P, KF, 2 * HEADS], F32, 96 * KIB + 256)
        wc = place("wc", [P, 2, 512], F32, 32 * KIB)
        attc = place("attc", [P, 2, 512], F32, 36 * KIB)
        prod = place("prod", [P, 512], F32, 40 * KIB)

        def attention_vectors(pool):
            s_wc, s_att, s_prod = [sem("v_w0"), sem("v_w1")], sem("v_att"), sem("v_prod")
            parts = [(ins[f"L1_gnn_W{n}"], ins[f"L1_gnn_att_src{n}"], ins[f"L1_gnn_att_dst{n}"], v, k, c)
                     for n, v, KI, F in ((1, v1, KD, F1), (2, v2, KF, HEADS * CH2))
                     for c in range(F // 512) for k in range(KI)]
            n, chunks = 0, 0

            def fetch(i):
                W_d, _, _, _, k, c = parts[i]
                pool.dma_start(wc[:, i % 2, :], W_d[k * P:(k + 1) * P, c * 512:(c + 1) * 512]).then_inc(s_wc[i % 2], 16)

            fetch(0)
            for i, (W_d, src, dst, v, k, c) in enumerate(parts):
                heads = 512 // src.shape[1]
                if k == 0:
                    chunks += 1
                    for a, d in enumerate((src, dst)):
                        pool.dma_start(attc[:, a, :], bcast(d.rearrange("h c -> (h c)")[c * 512:(c + 1) * 512], 512)
                                       ).then_inc(s_att, 16)
                    pool.wait_ge(s_att, 32 * chunks)
                if i + 1 < len(parts):
                    fetch(i + 1)
                pool.wait_ge(s_wc[i % 2], 16 * (i // 2 + 1))
                for a in range(2):
                    pool.tensor_tensor(prod[:], wc[:, i % 2, :], attc[:, a, :], ALU.mult).then_inc(s_prod, 1)
                    n += 1
                    pool.wait_ge(s_prod, n)
                    by = prod[:].rearrange("p (h c) -> p h c", h=heads)
                    width = 512 // heads
                    while width > 1:
                        width //= 2
                        to = by[:, :, 0:width] if width > 1 else                             v[:, k, a * HEADS + c * heads:a * HEADS + (c + 1) * heads].unsqueeze(2)
                        pool.tensor_tensor(to, by[:, :, 0:width], by[:, :, width:2 * width], ALU.add
                                           ).then_inc(s_prod, 1)
                        n += 1
                        pool.wait_ge(s_prod, n)

        w2h = place("w2h", [P, 2, HC, D], F32R, 168 * KIB)
        w2l = place("w2l", [P, 2, HC, D], F32R, 199 * KIB + 512)
        hTh = place("hTh", [P, 2, HC, P], F32R, 42 * KIB)
        hTl = place("hTl", [P, 2, HC, P], F32R, 44 * KIB)

        def experts(tag, blocks, table, W1_d, W2_d, b1_d, xs, ys, rows, loop, s_w, fetched, owner=None,
                    counts=None, beside=None):
            NX = b1_d.shape[0]
            HALF = P // 2
            s_clear = sem(tag + "_clear")

            def load_rows(sp, e, row, j):
                if counts is None:
                    sp.dma_start(xg[:, j, :], xs[bass.ds(row, P), :]).then_inc(s_xg[j], 16)
                    return
                sp.dma_start(xg[0:HALF, j, :], xs[bass.ds(row, HALF), :]).then_inc(s_xg[j], 16)
                n = first_row(sp, counts, e, P)
                with sp.If(n > HALF):
                    sp.dma_start(xg[HALF:P, j, :], xs[bass.ds(sp.snap(row + HALF), HALF), :]).then_inc(s_xg[j], 16)
                with sp.Else():
                    sp.sem_inc(s_xg[j], 16)
            s_xg = [sem(f"{tag}_xg{j}") for j in range(4)]
            s_ys = sem(tag + "_ys")
            s_t, s_tm, s_h, s_hm, s_y, s_ym = (sem(tag + "_" + k) for k in ("t", "tm", "h", "hm", "y", "ym"))
            s_hh, s_hl, s_wh, s_wl = (sem(f"{tag}_{k}") for k in ("hh", "hl", "wh", "wl"))
            s_b1, s_b1t, s_b1m = (sem(tag + "_" + k) for k in ("b1", "b1t", "b1m"))

            def expert(eng, e):
                if owner is not None:
                    return bass.ds(first_row(eng, owner, e, NX - 1), 1)
                return slice(e, e + 1) if isinstance(e, int) else bass.ds(e, 1)

            with nc.Block() as block:
                @block.gpsimd
                def _(pool):
                    pool.memset(xg[HALF:P, :, :], 0.0).then_inc(s_clear, 1)
                    pool.wait_ge(s_clear, 1)
                    if beside is not None:
                        beside(pool)

                @block.sync
                def _(sp):
                    sp.dma_start(b1s[0:NX, :], b1_d).then_inc(s_b1, 16)

                    def body(e, g, j, last):
                        wait(sp, s_y, e - 3)
                        row = first_row(sp, table, e, rows)
                        load_rows(sp, e, row, j)
                        if not fetched or not isinstance(e, int) or e >= 4:
                            load_weights(sp, W1_d, W2_d, expert(sp, e), j, s_w)

                    sp.wait_ge(s_clear, 1)
                    loop(sp, body)

                @block.tensor
                def _(pe):
                    pe.wait_ge(s_b1, 16)
                    for c in range(HC):
                        mm = pe.transpose(PS[:, 6, c * NX:(c + 1) * NX], b1s[0:NX, c * P:(c + 1) * P],
                                          ident[0:NX, 0:NX])
                    mm.then_inc(s_b1t, 1)

                    def turn(e, g, j):
                        pe.wait_ge(s_xg[j], (g + 1) * (16 if counts is None else 32))
                        wait(pe, s_tm, e - 1)
                        for k in range(KD):
                            mm = pe.transpose(PS[:, j % 2, k * P:(k + 1) * P], xg[:, j, k * P:(k + 1) * P], ident[:])
                        mm.then_inc(s_t, 1)

                    def hidden(e, g, j):
                        pe.wait_ge(s_w[j], (g + 1) * 32)
                        pe.wait_ge(s_tm, e + 1)
                        wait(pe, s_hm, e - 1)
                        for c in range(HC):
                            for k in range(KD):
                                mm = pe.matmul(PS[:, 2 + j % 2, c * P:(c + 1) * P], w1r[:, j, k, c * P:(c + 1) * P],
                                               xgT[:, j % 2, k, :], start=(k == 0), stop=(k == KD - 1))
                        mm.then_inc(s_h, 1)

                    def output(e, j):
                        pe.wait_ge(s_hl, e + 1)
                        pe.wait_ge(s_wl, e + 1)
                        wait(pe, s_ym, e - 1)
                        products = [(hp, wp, c) for hp, wp in ((hTh, w2h), (hTh, w2l), (hTl, w2h)) for c in range(HC)]
                        for n, (hp, wp, c) in enumerate(products):
                            mm = pe.matmul(PS[:, 4 + j % 2, :], hp[:, j % 2, c, :], wp[:, j % 2, c, :],
                                           start=(n == 0), stop=(n == len(products) - 1))
                        mm.then_inc(s_y, 1)

                    turn(0, 0, 0)

                    def body(e, g, j, last):
                        if not last:
                            turn(e + 1, g + 1 if j == 3 else g, (j + 1) % 4)
                        hidden(e, g, j)
                        if not (isinstance(e, int) and e == 0):
                            output(e - 1, (j + 3) % 4)

                    loop(pe, body)
                    output(blocks - 1, (blocks - 1) % 4)

                @block.scalar
                def _(act):
                    act.wait_ge(s_b1t, 1)
                    act.copy(b1T[:, :, 0:NX], PS[:, 6, 0:HC * NX].rearrange("p (c e) -> p c e", c=HC)).then_inc(s_b1m, 1)
                    act.wait_ge(s_b1m, 1)

                    def body(e, g, j, last):
                        col = expert(act, e)
                        act.wait_ge(s_h, e + 1)
                        wait(act, s_y, e - 1)
                        for c in range(HC):
                            a = act.activation(hT[:, j % 2, c, :], PS[:, 2 + j % 2, c * P:(c + 1) * P], ACT.Relu,
                                               bias=b1T[:, c, col])
                        a.then_inc(s_hm, 1)
                        act.wait_ge(s_hm, e + 1)
                        act.copy(hTh[:, j % 2, :, :], hT[:, j % 2, :, :]).then_inc(s_hh, 1)
                        if not last:
                            upper(e + 1, g + 1 if j == 3 else g, (j + 1) % 4)
                        if not (isinstance(e, int) and e == 0):
                            store(e - 1, (j + 3) % 4)

                    def upper(e, g, j):
                        act.wait_ge(s_w[j], (g + 1) * 32)
                        wait(act, s_y, e - 1)
                        act.copy(w2h[:, j % 2, :, :], w2r[:, j, :, :]).then_inc(s_wh, 1)

                    def store(e, j):
                        e = e if isinstance(e, int) else within(act.snap(e), 0, blocks - 1)
                        row = first_row(act, table, e, rows)
                        act.wait_ge(s_ym, e + 1)
                        wait(act, s_ys, 16 * (e + 1))
                        act.dma_start(ys[bass.ds(row, P), :], yo[:, j, :]).then_inc(s_ys, 16)

                    act.sem_inc(s_ys, 16)
                    upper(0, 0, 0)
                    loop(act, body)
                    store(blocks - 1, (blocks - 1) % 4)
                    act.wait_ge(s_ys, 16 * (blocks + 1))

                @block.vector
                def _(dve):
                    def turned(e, j):
                        dve.wait_ge(s_t, e + 1)
                        wait(dve, s_h, e - 1)
                        dve.tensor_copy(xgT[:, j % 2, :, :].rearrange("p k n -> p (k n)"), PS[:, j % 2, :]
                                        ).then_inc(s_tm, 1)

                    def moved(e, g, j):
                        dve.wait_ge(s_y, e + 1)
                        wait(dve, s_ys, 16 * (e - 2))
                        dve.tensor_copy(yo[:, j, :], PS[:, 4 + j % 2, :]).then_inc(s_ym, 1)

                    def lower(e, g, j):
                        dve.wait_ge(s_wh, e + 1)
                        dve.tensor_tensor(w2l[:, j % 2, :, :], w2r[:, j, :, :], w2h[:, j % 2, :, :].bitcast(F32),
                                          ALU.subtract).then_inc(s_wl, 1)

                    turned(0, 0)
                    lower(0, 0, 0)

                    def body(e, g, j, last):
                        if not last:
                            turned(e + 1, (j + 1) % 4)
                        if not (isinstance(e, int) and e == 0):
                            moved(e - 1, g if j else g - 1, (j + 3) % 4)
                        dve.wait_ge(s_hh, e + 1)
                        dve.tensor_tensor(hTl[:, j % 2, :, :], hT[:, j % 2, :, :], hTh[:, j % 2, :, :].bitcast(F32),
                                          ALU.subtract).then_inc(s_hl, 1)
                        if not last:
                            lower(e + 1, g, (j + 1) % 4)

                    loop(dve, body)
                    moved(blocks - 1, (blocks - 1) // 4, (blocks - 1) % 4)

        phase()
        experts("x0", NX0, offi, ins["L0_ffn_W1"], ins["L0_ffn_W2"], ins["L0_ffn_b1"], xs_dram[0], ys_dram[0],
                N * TOPK, loop, s_w0, True, None, r0["firsti"],
                attention_vectors)

        NO0 = NB0 - NX0
        phase()
        s_next, s_w, s_xg, s_ys = (sem("x1_" + k) for k in ("next", "w", "xg", "ys"))
        s_t, s_tm, s_h, s_hm, s_y, s_ym = (sem("x1_" + k) for k in ("t", "tm", "h", "hm", "y", "ym"))
        with nc.Block() as block:
            def each(eng, body):
                more = eng.value_load(owni[0:1, NO0:NO0 + 1], min_val=0, max_val=NO0)
                with eng.If(more > 0):
                    with eng.Fori(0, more) as j:
                        eng.wait_ge(s_next, j + 1)
                        body(j)

            @block.sync
            def _(sp):
                def body(j):
                    e = sp.value_load(owni[0:1, bass.ds(j, 1)], min_val=0, max_val=NX0 - 1)
                    row = first_row(sp, starti, j, N * TOPK)
                    sp.dma_start(xg[:, 0, :], xs_dram[0][bass.ds(row, P), :]).then_inc(s_xg, 16)
                    sp.dma_start(w1r[:, 0, :, :], ins["L0_ffn_W1"][bass.ds(e, 1)].rearrange(
                        "o (k p) h -> p (o k) h", p=P)).then_inc(s_w, 16)
                    sp.dma_start(w2r[:, 0, :, :], ins["L0_ffn_W2"][bass.ds(e, 1)].rearrange(
                        "o (k p) h -> p (o k) h", p=P)).then_inc(s_w, 16)
                    sp.wait_ge(s_ym, j + 1)
                    sp.dma_start(ys_dram[0][bass.ds(row, P), :], yo[:, 0, :]).then_inc(s_ys, 16)
                    sp.wait_ge(s_ys, (j + 1) * 16)
                    sp.sem_inc(s_next, 1)

                sp.sem_inc(s_next, 1)
                each(sp, body)

            @block.tensor
            def _(pe):
                def body(j):
                    pe.wait_ge(s_xg, (j + 1) * 16)
                    for k in range(KD):
                        mm = pe.transpose(PS[:, 0, k * P:(k + 1) * P], xg[:, 0, k * P:(k + 1) * P], ident[:])
                    mm.then_inc(s_t, 1)
                    pe.wait_ge(s_w, (j + 1) * 32)
                    pe.wait_ge(s_tm, j + 1)
                    for c in range(HC):
                        for k in range(KD):
                            mm = pe.matmul(PS[:, 2, c * P:(c + 1) * P], w1r[:, 0, k, c * P:(c + 1) * P],
                                           xgT[:, 0, k, :], start=(k == 0), stop=(k == KD - 1))
                    mm.then_inc(s_h, 1)
                    pe.wait_ge(s_hm, j + 1)
                    for c in range(HC):
                        mm = pe.matmul(PS[:, 4, :], hT[:, 0, c, :], w2r[:, 0, c, :], start=(c == 0),
                                       stop=(c == HC - 1))
                    mm.then_inc(s_y, 1)

                each(pe, body)

            @block.scalar
            def _(act):
                def body(j):
                    e = act.value_load(owni[0:1, bass.ds(j, 1)], min_val=0, max_val=NX0 - 1)
                    act.wait_ge(s_h, j + 1)
                    for c in range(HC):
                        a = act.activation(hT[:, 0, c, :], PS[:, 2, c * P:(c + 1) * P], ACT.Relu,
                                           bias=b1T[:, c, bass.ds(e, 1)])
                    a.then_inc(s_hm, 1)

                each(act, body)

            @block.vector
            def _(dve):
                def body(j):
                    dve.wait_ge(s_t, j + 1)
                    dve.tensor_copy(xgT[:, 0, :, :].rearrange("p k n -> p (k n)"), PS[:, 0, :]).then_inc(s_tm, 1)
                    dve.wait_ge(s_y, j + 1)
                    dve.tensor_copy(yo[:, 0, :], PS[:, 4, :]).then_inc(s_ym, 1)

                each(dve, body)

        yb = place("yb", [P, 4, TOPK, D], F32, 152 * KIB)
        o0 = place("o0", [P, NT, D], F32, 120 * KIB)
        shift = place("shift", [P, NT], F32, 151 * KIB)
        gamma = place("gamma", [P, D], F32, 136 * KIB)
        beta = place("beta", [P, D], F32, 138 * KIB)
        phase()
        s_yb, s_gb = [sem(f"c0_yb{j}") for j in range(4)], sem("c0_gb")
        s_bias, s_sum, s_stat, s_sqrt, s_chain = (sem("c0_" + k) for k in ("bias", "sum", "stat", "sqrt", "chain"))
        s_scale, s_norm, s_beta, s_scaled = (sem("c0_" + k) for k in ("scale", "norm", "beta", "scaled"))
        with nc.Block() as block:
            @block.sync
            def _(sp):
                sp.dma_start(gamma[:], bcast(ins["L0_ffn_gamma"], D)).then_inc(s_gb, 16)
                sp.dma_start(beta[:], bcast(ins["L0_ffn_beta"], D)).then_inc(s_gb, 16)

            @block.gpsimd
            def _(pool):
                for t in range(NT):
                    if t >= 4:
                        pool.wait_ge(s_sum, t - 3)
                    for k in range(TOPK):
                        pool.indirect_dma_start(yb[:, t % 4, k, :], None, ys_dram[0][0:N * TOPK, :], bass.IndirectOffsetOnAxis(
                            r0["posi"][:, t, k:k + 1], 0)).then_inc(s_yb[t % 4], 16)
                pool.wait_ge(s_gb, 32)
                for t in range(NT):
                    pool.tensor_tensor(x[:, t, :], x[:, t, :], beta[:], ALU.add).then_inc(s_beta, 1)

            @block.tensor
            def _(pe):
                for t in range(NT):
                    if t >= 4:
                        pe.wait_ge(s_sum, t - 3)
                    pe.matmul(PS[:, t % 4, :], r0["swT"][:, t * P:(t + 1) * P], r0["b2s"][:], start=True,
                              stop=True).then_inc(s_bias, 1)

            @block.scalar
            def _(act):
                act.wait_ge(s_stat, 1)
                act.activation(sq[:], ve[:], ACT.Sqrt).then_inc(s_sqrt, 1)
                act.wait_ge(s_scale, 1)
                for t in range(NT):
                    act.activation(o0[:, t, :], o0[:, t, :], ACT.Identity, bias=shift[:, t:t + 1],
                                   scale=rs[:, t:t + 1]).then_inc(s_norm, 1)

            @block.vector
            def _(dve):
                n = [0]

                def link(ins):
                    n[0] += 1
                    ins.then_inc(s_chain, 1)
                    dve.wait_ge(s_chain, n[0])

                top = r0["top"]
                for t in range(NT):
                    dve.wait_ge(s_bias, t + 1)
                    dve.wait_ge(s_yb[t % 4], 32 * (t // 4 + 1))
                    link(dve.tensor_tensor(o0[:, t, :], PS[:, t % 4, :], xln[:, t, :], ALU.add))
                    link(dve.scalar_tensor_tensor(o0[:, t, :], yb[:, t % 4, 0, :], top[:, t, 0:1], o0[:, t, :],
                                                  ALU.mult, ALU.add))
                    dve.scalar_tensor_tensor(o0[:, t, :], yb[:, t % 4, 1, :], top[:, t, 1:2], o0[:, t, :],
                                             ALU.mult, ALU.add).then_inc(s_sum, 1)
                    dve.wait_ge(s_sum, t + 1)
                    link(dve.bn_stats(st[:, t, :], o0[:, t, :]))
                    last = dve.bn_aggr(mv[:, t, :], st[:, t, :])
                link(last)
                dve.tensor_scalar(ve[:], mv[:, :, 1], LN_EPS, None, ALU.add).then_inc(s_stat, 1)
                dve.wait_ge(s_sqrt, 1)
                link(dve.reciprocal(tq[:], sq[:]))
                link(dve.tensor_tensor(tq[:], tq[:], ve[:], ALU.mult))
                link(dve.tensor_tensor(tq[:], tq[:], sq[:], ALU.add))
                link(dve.tensor_scalar(tq[:], tq[:], 0.5, None, ALU.mult))
                link(dve.reciprocal(rs[:], tq[:]))
                dve.scalar_tensor_tensor(shift[:], mv[:, :, 0], -1.0, rs[:], ALU.mult, ALU.mult).then_inc(s_scale, 1)
                dve.wait_ge(s_gb, 32)
                dve.wait_ge(s_beta, NT)
                for t in range(NT + 1):
                    if t < NT:
                        dve.wait_ge(s_norm, t + 1)
                        dve.tensor_tensor(o0[:, t, :], o0[:, t, :], gamma[:], ALU.mult).then_inc(s_scaled, 1)
                    if t:
                        dve.wait_ge(s_scaled, t)
                        last = dve.tensor_tensor(x[:, t - 1, :], x[:, t - 1, :], o0[:, t - 1, :], ALU.add)
                link(last)

        RING = 8
        x2T = place("x2T", [P, KF, N], F32, 16 * KIB)
        ab = place("ab", [P, NT, 2 * HEADS], F32, 96 * KIB + 768)
        as02 = place("as02", [P, NT, HEADS], F32, 97 * KIB + 256)
        b1T2 = place("b1T2", [P, HEADS], F32, 97 * KIB + 512)
        dn = place("dn", [P, 12], F32, 97 * KIB + 544)
        rd = place("rd", [P, 12], F32, 97 * KIB + 608)
        spare = place("spare", [P, HEADS], F32, 97 * KIB + 672)
        mrow = place("mrow", [P, 2, NT], F32, 97 * KIB + 704)
        zx = place("zx", [P, NT], F32, 97 * KIB + 768)
        q4 = place("q4", [P, 2, NT], F32, 97 * KIB + 800)
        asb = place("asb", [P, N], F32, 102 * KIB)
        masked = place("masked", [P, N], F32, 106 * KIB)
        am = place("am", [P, RING, N], F32, 145 * KIB)
        aTs = place("aTs", [2 * HEADS, N], F32, 173 * KIB)
        PT = place("PT", [P, 2, N], F32, 177 * KIB)
        adb = place("adb", [P, 2, N], F32, 185 * KIB)
        qb = place("qb", [P, 2, N], F32, 193 * KIB)
        o1 = place("o1", [P, 9, CH1], F32, 201 * KIB)

        def attend(tag, KI, CH, xT, W, W_d, v, h, bias_d, adr, qdr, final):
            F = HEADS * CH
            FH = F // 2
            PER = min(512 // (CH + 1), 4)
            NBK = -(-NT // PER)
            SLOPE = 1 / NEG_SLOPE
            MAXED = {1: (0, 1), 2: (2, 3), 3: (4,), 4: (5,), 5: (6,), 6: (7,)}
            H_UNITS = tuple(range(NT)) if final else (0, 2, 3, 5, 7, 8, 10, 12)
            if final:
                bias = place(tag + "_bias", [P, F], F32, 133 * KIB)
                zo = place(tag + "_zo", [P, NT, F], F32, 16 * KIB)
                zt = place(tag + "_zt", [P, 2, F], F32, 135 * KIB)
                hs = place(tag + "_hs", [P, 2, NT, CH + 1], F32, 201 * KIB)
                oT = place(tag + "_oT", [CH + 1, N], F32, 129 * KIB)
            s_in, s_w = [sem(f"{tag}_rows{j}") for j in range(2)], [sem(f"{tag}_w{j}") for j in range(2)]
            s_a, s_am, s_row, s_b, s_bm, s_h, s_hm, s_ones, s_as, s_max, s_q, s_qc, s_qrow = (
                sem(f"{tag}_{k}") for k in ("a", "am", "row", "b", "bm", "h", "hm", "ones", "as", "max", "q", "qc",
                                            "qrow"))
            s_bias, s_relu, s_sum, s_all, s_exp, s_O, s_ev, s_tr, s_xm, s_chain = (
                sem(f"{tag}_{k}") for k in ("bias", "relu", "sum", "scores", "exp", "O", "ev", "tr", "xm", "chain"))
            s_hs, s_oT, s_z, s_ze, s_ln = (sem(f"{tag}_{k}") for k in ("hs", "oT", "z", "ze", "ln"))
            early = [asb[:], am[:, 6, :]]

            def pairs(eng, body):
                body(0, False)
                with eng.Fori(1, HEADS // 2 - 1) as g:
                    body(g, False)
                body(HEADS // 2 - 1, True)

            def one(h):
                return slice(h, h + 1) if isinstance(h, int) else bass.ds(h, 1)

            def of(tensor, s, h):
                return tensor[:, s, h:h + 1] if isinstance(h, int) else tensor[:, s, bass.ds(h, 1)]

            def ahead(g, k, d, last):
                if k + d < 2 * NT:
                    return g, k + d
                return None if last else (g + 1, k + d - 2 * NT)

            def first(g, k):
                return isinstance(g, int) and g == 0 and k < NT

            with nc.Block() as block:
                @block.sync
                def _(sp):
                    for half in range(2):
                        sp.dma_start(W[:, :, half * FH:(half + 1) * FH], W_d.rearrange(
                            "(k p) n -> p k n", p=P)[:, :, half * FH:(half + 1) * FH]).then_inc(s_w[half], 16)
                    if not final:
                        with nc.allow_non_contiguous_dma(reason="one value per head and partition"):
                            sp.dma_start(b1T2[:], bias_d.rearrange("(h c) -> c h", c=CH)).then_inc(s_bias, 16)
                    sp.wait_ge(s_am, 1)
                    sp.dma_start(adr, aTs[:]).then_inc(s_row, 16)
                    sp.wait_ge(s_row, 16)
                    sp.dma_start(early[0], bcast(adr[0], N)).then_inc(s_as, 16)
                    sp.wait_ge(s_as, 16)
                    sp.dma_start(early[1], bcast(adr[1], N)).then_inc(s_as, 16)
                    sp.wait_ge(s_as, 32)
                    for hd in range(HEADS):
                        sp.wait_ge(s_q, hd + 1)
                        with nc.allow_non_contiguous_dma(reason="one value per tile and partition"):
                            sp.dma_start(qdr[hd].rearrange("(t p) -> p t", p=P), q4[:, hd % 2, :]).then_inc(s_qrow, 16)
                        if hd >= 1 and hd + 1 < HEADS:
                            sp.dma_start(asb[:], bcast(adr[hd + 1], N)).then_inc(s_as, 16)
                        sp.wait_ge(s_qrow, 16 * (hd + 1))
                        if hd >= 2:
                            sp.wait_ge(s_exp, NT * (hd - 1))
                        sp.dma_start(adb[:, hd % 2, :], bcast(adr[HEADS + hd], N)).then_inc(s_in[hd % 2], 16)
                        sp.dma_start(qb[:, hd % 2, :], bcast(qdr[hd], N)).then_inc(s_in[hd % 2], 16)
                        if final and hd == 2:
                            sp.wait_ge(s_hm, 2 * NT)
                            sp.dma_start(bias[:], bcast(bias_d, F)).then_inc(s_bias, 16)

                def rows_in(eng, g, k):
                    eng.wait_ge(s_in[k // NT], (g + 1) * 32)

                @block.scalar
                def _(act):
                    def relu(g, k):
                        if k % NT == 0:
                            rows_in(act, g, k)
                        wait(act, s_exp, 16 * g + k - RING + 1)
                        act.activation(am[:, k % RING, :], adb[:, k // NT, :], ACT.Relu, bias=of(ab, k % NT, 2 * g + k // NT)
                                       ).then_inc(s_relu, 1)

                    def exp(g, k):
                        act.wait_ge(s_all, 16 * g + k + 1)
                        wait(act, s_O, 16 * g + k - 1)
                        act.activation(PT[:, k % 2, :], am[:, k % RING, :], ACT.Exp, bias=of(as02, k % NT, 2 * g + k // NT),
                                       scale=1 - NEG_SLOPE).then_inc(s_exp, 1)

                    def moved(hd, parity):
                        act.wait_ge(s_O, NT * hd + NT)
                        wait(act, s_tr, hd)
                        act.copy(oT[:], PS[0:CH + 1, 2 * parity:2 * parity + 2, :].rearrange("p a n -> p (a n)")
                                 ).then_inc(s_oT, 1)

                    def out(hd):
                        act.wait_ge(s_tr, hd + 1)
                        act.activation(x2T[:, one(hd), :].rearrange("p o n -> p (o n)"),
                                       PS[:, 6:8, :].rearrange("p a n -> p (a n)"), ACT.Relu,
                                       bias=b1T2[:, one(hd)]).then_inc(s_xm, 1)

                    def h_moved(half, t, bank):
                        act.wait_ge(s_h, half * NT + t + 1)
                        act.copy(h[:, t, half * HEADS // 2:(half + 1) * HEADS // 2, 0:CH],
                                 PS[:, bank, 0:FH].rearrange("p (h c) -> p h c", c=CH)).then_inc(s_hm, 1)

                    def body(g, last):
                        for k in range(2 * NT):
                            if u := ahead(g, k, 6, last):
                                relu(*u)
                            exp(g, k)
                            if isinstance(g, int) and g == 0 and k in H_UNITS:
                                h_moved(1, H_UNITS.index(k), 7)
                            if final and k % NT == 2 and not first(g, k):
                                moved(2 * g + k // NT - 1, (k // NT + 1) % 2)
                            if not final and k % NT == 1 and not (isinstance(g, int) and g == 0):
                                out(2 * g + k // NT - 2)

                    act.wait_ge(s_a, 1)
                    act.copy(aTs[:], PS[0:2 * HEADS, 4:6, :].rearrange("p a n -> p (a n)")).then_inc(s_am, 1)
                    for t in range(NT):
                        h_moved(0, t, t % 2)
                    if not final:
                        act.wait_ge(s_bias, 16)
                    act.wait_ge(s_row, 16)
                    act.wait_ge(s_b, 1)
                    act.wait_ge(s_max, 2 * NT)
                    for k in range(6):
                        relu(0, k)
                    pairs(act, body)
                    if not final:
                        out(HEADS - 2)
                        out(HEADS - 1)
                    else:
                        moved(HEADS - 1, 1)
                        for t in range(NT):
                            act.wait_ge(s_z, t + 1)
                            act.activation(zt[:, t % 2, :], zo[:, t, :], ACT.Exp, bias=nmt[:, t:t + 1],
                                           accum_out=sq[:, t:t + 1]).then_inc(s_ze, 1)
                            act.wait_ge(s_ze, t + 1)
                        act.activation(ve[:], sq[:], ACT.Ln).then_inc(s_ln, 1)

                @block.gpsimd
                def _(pool):
                    pool.memset(h[:, :, :, CH:CH + 1], 1.0).then_inc(s_ones, 1)

                    def staged(hd, parity):
                        wait(pool, s_O, NT * (hd - 1))
                        pool.tensor_copy(hs[:, parity, :, :], h[:, :, one(hd), :].rearrange("p t o c -> p (t o) c")
                                         ).then_inc(s_hs, 1)

                    if final:
                        pool.wait_ge(s_ones, 1)
                        pool.wait_ge(s_hm, NT)
                        staged(0, 0)

                    def body(g, last):
                        for k in range(2 * NT):
                            if k % NT == 0:
                                rows_in(pool, g, k)
                            if final and k % NT == 5 and not (last and k > NT):
                                if isinstance(g, int) and g == 0 and k > NT:
                                    pool.wait_ge(s_hm, 2 * NT)
                                staged(2 * g + k // NT + 1, (k // NT + 1) % 2)
                            pool.wait_ge(s_relu, 16 * g + k + 1)
                            pool.tensor_tensor(am[:, k % RING, :], am[:, k % RING, :], qb[:, k // NT, :], ALU.add
                                               ).then_inc(s_sum, 1)

                    pairs(pool, body)

                @block.vector
                def _(dve):
                    def link(ins, n, s=s_chain):
                        ins.then_inc(s, 1)
                        dve.wait_ge(s, n)

                    def maxed(hd, t, parity, rows):
                        if t == 0:
                            dve.wait_ge(s_as, 16 * (hd + 1))
                        wait(dve, s_max, NT * hd + t)
                        dve.memset(spare[:, t:t + 1], 0.0)
                        dve.tensor_tensor_reduce(masked[:], rows, mask[:, t, :], 1.0, -3.0e38, ALU.add, ALU.max,
                                                 mrow[:, parity, t:t + 1]).then_inc(s_max, 1)

                    def q(hd, parity):
                        dve.wait_ge(s_max, NT * hd + NT)
                        a_dst = ab[:, :, HEADS + hd:HEADS + hd + 1] if isinstance(hd, int) else \
                            ab[:, :, bass.ds(HEADS + hd, 1)]
                        a_dst = a_dst.rearrange("p t o -> p (t o)")
                        link(dve.tensor_tensor(zx[:], mrow[:, parity, :], a_dst, ALU.add), 3 * hd + 1, s_qc)
                        link(dve.scalar_tensor_tensor(zx[:], zx[:], SLOPE, zx[:], ALU.mult, ALU.max), 3 * hd + 2, s_qc)
                        link(dve.tensor_tensor(zx[:], a_dst, zx[:], ALU.subtract), 3 * hd + 3, s_qc)
                        wait(dve, s_qrow, 16 * (hd - 1))
                        dve.tensor_scalar(q4[:, parity, :], zx[:], 1 / (SLOPE - 1), None, ALU.mult).then_inc(s_q, 1)

                    def counted(g, k):
                        dve.wait_ge(s_sum, 16 * g + k + 1)
                        dve.tensor_tensor(am[:, k % RING, :], am[:, k % RING, :], CT[:, k % NT, :], ALU.add
                                          ).then_inc(s_all, 1)

                    def normed(hd, parity):
                        if final:
                            dve.wait_ge(s_tr, hd + 1)
                            parity = 2
                        else:
                            dve.wait_ge(s_O, NT * hd + NT)
                        O = PS[:, parity * NBK:(parity + 1) * NBK, 0:PER * (CH + 1)].rearrange(
                            "p b (t c) -> p b t c", c=CH + 1)
                        link(dve.tensor_scalar(dn[:, 0:NBK * PER].rearrange("p (b t) -> p b t", t=PER), O[:, :, :, CH],
                                               1e-16, None, ALU.add), 2 * hd + 1)
                        link(dve.reciprocal(rd[:, 0:NBK * PER], dn[:, 0:NBK * PER]), 2 * hd + 2)
                        scale = rd[:, 0:NBK * PER].rearrange("p (b t) -> p b t", t=PER).unsqueeze(3).to_broadcast(
                            [P, NBK, PER, CH])
                        if final:
                            dst = zo[:, :, hd * CH:(hd + 1) * CH] if isinstance(hd, int) else \
                                zo[:, :, bass.ds(hd * CH, CH)]
                        else:
                            wait(dve, s_tr, hd)
                            dst = o1[:, 0:NBK * PER, :]
                        dve.tensor_tensor(dst.rearrange("p (b t) c -> p b t c", t=PER), O[:, :, :, 0:CH], scale,
                                          ALU.mult).then_inc(s_ev, 1)

                    def body(g, last):
                        for k in range(2 * NT):
                            parity = k // NT
                            if not last:
                                for t in MAXED.get(k % NT, ()):
                                    maxed(2 * g + parity + 2, t, parity, asb[:])
                                if k % NT == 6:
                                    q(2 * g + parity + 2, parity)
                            counted(g, k)
                            if k % NT == (7 if final else 7) and not first(g, k):
                                normed(2 * g + parity - 1, (parity + 1) % 2)

                    dve.wait_ge(s_b, 1)
                    dve.tensor_copy(ab[:].rearrange("p t h -> p (t h)"), PS[:, 6, 0:NT * 2 * HEADS]).then_inc(s_bm, 1)
                    dve.wait_ge(s_bm, 1)
                    dve.tensor_scalar(as02[:], ab[:, :, 0:HEADS], NEG_SLOPE, None, ALU.mult)
                    for hd in range(2):
                        for t in range(NT):
                            maxed(hd, t, hd, early[hd])
                        q(hd, hd)
                    pairs(dve, body)
                    normed(HEADS - 1, 1)
                    if final:
                        dve.wait_ge(s_ev, HEADS)
                        dve.wait_ge(s_bias, 16)
                        n = 2 * HEADS
                        for t in range(NT):
                            n += 2
                            link(dve.tensor_tensor(zo[:, t, :], zo[:, t, :], bias[:], ALU.add), n - 1)
                            link(dve.tensor_reduce(dn[:, 0:1], zo[:, t, :], X, ALU.max), n)
                            dve.tensor_scalar(nmt[:, t:t + 1], dn[:, 0:1], -1.0, None, ALU.mult).then_inc(s_z, 1)
                            dve.wait_ge(s_z, t + 1)
                        dve.wait_ge(s_ln, 1)
                        link(dve.tensor_tensor(ve[:], ve[:], nmt[:], ALU.subtract), n + 1)
                        for t in range(NT):
                            last = dve.scalar_tensor_tensor(x[:, t, :], zo[:, t, :], ve[:, t:t + 1], x[:, t, :],
                                                            ALU.subtract, ALU.add)
                        link(last, n + 2)

                @block.tensor
                def _(pe):
                    for half in range(2):
                        for k in range(KI):
                            mm = pe.matmul(PS[0:2 * HEADS, 4 + half, :], v[:, k, :], xT[:, k, half * 512:(half + 1) * 512],
                                           start=(k == 0), stop=(k == KI - 1))
                    mm.then_inc(s_a, 1)
                    pe.wait_ge(s_am, 1)
                    for t in range(NT):
                        mm = pe.transpose(PS[:, 6, t * 2 * HEADS:(t + 1) * 2 * HEADS], aTs[:, t * P:(t + 1) * P],
                                          ident[0:2 * HEADS, 0:2 * HEADS])
                    mm.then_inc(s_b, 1)

                    def h_tile(half, t, bank):
                        for k in range(KI):
                            mm = pe.matmul(PS[:, bank, 0:FH], xT[:, k, t * P:(t + 1) * P],
                                           W[:, k, half * FH:(half + 1) * FH], start=(k == 0), stop=(k == KI - 1))
                        mm.then_inc(s_h, 1)

                    pe.wait_ge(s_w[0], 16)
                    for t in range(NT):
                        wait(pe, s_hm, t - 1)
                        h_tile(0, t, t % 2)
                    pe.wait_ge(s_w[1], 16)
                    pe.wait_ge(s_hm, NT)
                    pe.wait_ge(s_ones, 1)

                    def gather(g, k):
                        s, parity = k % NT, k // NT
                        if s == 0:
                            wait(pe, s_ev, 2 * g + parity - 1)
                            for b in range(NBK):
                                pe.matmul(PS[:, parity * NBK + b, 0:PER * (CH + 1)], onesb[:], zerob[:, 0:PER * (CH + 1)],
                                          start=True, stop=False)
                        pe.wait_ge(s_exp, 16 * g + k + 1)
                        moving = h[:, s, one(2 * g + parity), :].rearrange("p o c -> p (o c)")
                        for d in range(NT):
                            mm = pe.matmul(PS[:, parity * NBK + d // PER, (d % PER) * (CH + 1):(d % PER + 1) * (CH + 1)],
                                           PT[:, k % 2, d * P:(d + 1) * P], moving, start=False,
                                           stop=(s == NT - 1 and d in (NT - 1, *range(PER - 1, NT, PER))))
                        mm.then_inc(s_O, 1)

                    def columns(g, k):
                        s, parity = k % NT, k // NT
                        if s == 0:
                            pe.wait_ge(s_hs, 2 * g + parity + 1)
                            wait(pe, s_oT, 2 * g + parity - 1)
                        pe.wait_ge(s_exp, 16 * g + k + 1)
                        for half in range(2):
                            mm = pe.matmul(PS[0:CH + 1, 2 * parity + half, :], hs[:, parity, s, :],
                                           PT[:, k % 2, half * 512:(half + 1) * 512], start=(s == 0),
                                           stop=(s == NT - 1))
                        mm.then_inc(s_O, 1)

                    def rows(hd):
                        pe.wait_ge(s_oT, hd + 1)
                        wait(pe, s_ev, hd)
                        for d in range(NT):
                            mm = pe.transpose(PS[:, 2 * NBK + d // PER, (d % PER) * (CH + 1):(d % PER + 1) * (CH + 1)],
                                              oT[:, d * P:(d + 1) * P], ident[0:CH + 1, 0:CH + 1])
                        mm.then_inc(s_tr, 1)

                    def turned(hd):
                        pe.wait_ge(s_ev, hd + 1)
                        wait(pe, s_xm, hd)
                        for d in range(NT):
                            mm = pe.transpose(PS[:, 6 + d // 4, (d % 4) * P:(d % 4 + 1) * P], o1[:, d, :], ident[:])
                        mm.then_inc(s_tr, 1)

                    def body(g, last):
                        for k in range(2 * NT):
                            if isinstance(g, int) and g == 0 and k in H_UNITS:
                                wait(pe, s_hm, NT + H_UNITS.index(k))
                                h_tile(1, H_UNITS.index(k), 7)
                            columns(g, k) if final else gather(g, k)
                            if final and k % NT == 4 and not first(g, k):
                                rows(2 * g + k // NT - 1)
                            if not final and k % NT == 7 and not first(g, k):
                                if isinstance(g, int) and g == 0:
                                    pe.wait_ge(s_hm, 2 * NT)
                                turned(2 * g + k // NT - 1)

                    pairs(pe, body)
                    rows(HEADS - 1) if final else turned(HEADS - 1)

        phase()
        layernorm("ln2", x, xln, xT)
        h1 = place("h1", [P, NT, HEADS, CH1 + 1], F32, 112 * KIB)
        W1t = place("W1t", [P, KD, F1], F32, 16 * KIB)
        phase()
        attend("a1", KD, CH1, xT, W1t, ins["L1_gnn_W1"], v1, h1, ins["L1_gnn_b1"], a_dram[0], q_dram[0], False)
        h2 = place("h2", [P, NT, HEADS, CH2 + 1], F32, 112 * KIB)
        W2t = place("W2t", [P, KF, HEADS * CH2], F32, 129 * KIB)
        phase()
        attend("a2", KF, CH2, x2T, W2t, ins["L1_gnn_W2"], v2, h2, ins["L1_gnn_b2"], a_dram[1], q_dram[1], True)

        xln3 = place("xln3", [P, NT, D], F32, 48 * KIB)
        xT3 = place("xT3", [P, KD, N], F32, 64 * KIB)
        r1 = router_buffers("r1", NX1, 1, NB1, True, 176 * KIB)
        assert r1["end"] <= ARENA
        phase()
        layernorm("ln3", x, xln3, xT3)
        phase()
        routing("rt1", NX1, 1, ins["L1_ffn_Wr"], ins["L1_ffn_br"], ins["L1_ffn_b2"], True, NB1,
                xs_dram[1], xln3, xT3, r1, lambda sp: None)
        def straight(eng, body):
            for n in range(NB1):
                body(n, n // 4, n % 4, n == NB1 - 1)

        phase()
        experts("x2", NB1, r1["starti"], ins["L1_ffn_W1"], ins["L1_ffn_W2"], ins["L1_ffn_b1"], xs_dram[1],
                ys_dram[1], N, straight, s_w1, False, r1["owni"])

        zb = place("zb", [P, NT, D], F32, 130 * KIB)
        phase()
        s_zb, s_bias, s_sum, s_add, s_out = [sem(f"f_zb{t}") for t in range(NT)], sem("f_bias"), sem("f_sum"), sem("f_add"), sem("f_out")
        with nc.Block() as block:
            @block.sync
            def _(sp):
                for t in range(NT):
                    sp.wait_ge(s_add, t + 1)
                    sp.dma_start(out[t * P:(t + 1) * P, :], x[:, t, :]).then_inc(s_out, 16)
                sp.wait_ge(s_out, 16 * NT)

            @block.gpsimd
            def _(pool):
                for t in range(NT):
                    pool.indirect_dma_start(zb[:, t, :], None, ys_dram[1][0:N, :],
                                            bass.IndirectOffsetOnAxis(r1["posi"][:, t, 0:1], 0)).then_inc(s_zb[t], 16)

            @block.tensor
            def _(pe):
                for t in range(NT):
                    pe.matmul(PS[:, t, :], r1["swT"][:, t * P:(t + 1) * P], r1["b2s"][:], start=True, stop=True
                              ).then_inc(s_bias, 1)

            @block.vector
            def _(dve):
                for t in range(NT):
                    dve.wait_ge(s_zb[t], 16)
                    dve.wait_ge(s_bias, t + 1)
                    dve.tensor_tensor(zb[:, t, :], zb[:, t, :], PS[:, t, :], ALU.add).then_inc(s_sum, 1)
                    dve.wait_ge(s_sum, t + 1)
                    dve.scalar_tensor_tensor(x[:, t, :], zb[:, t, :], r1["gate"][:, t:t + 1], x[:, t, :],
                                             ALU.mult, ALU.add).then_inc(s_add, 1)



_NAMES = ["x", "src", "dst", "L0_gnn_W", "L0_gnn_b", "L0_gnn_diffusion_weights", "L0_ffn_Wg", "L0_ffn_bg",
          "L0_ffn_W1", "L0_ffn_b1", "L0_ffn_W2", "L0_ffn_b2", "L0_ffn_gamma", "L0_ffn_beta", "L1_gnn_W1",
          "L1_gnn_att_src1", "L1_gnn_att_dst1", "L1_gnn_b1", "L1_gnn_W2", "L1_gnn_att_src2", "L1_gnn_att_dst2",
          "L1_gnn_b2", "L1_ffn_Wr", "L1_ffn_br", "L1_ffn_W1", "L1_ffn_b1", "L1_ffn_W2", "L1_ffn_b2"]


def kernel(**inputs):
    import numpy as np
    import concourse.bacc as bacc
    from concourse.bass_utils import run_bass_kernel_spmd

    nc = bacc.Bacc("TRN2", target_bir_lowering=False, num_devices=1)
    arrays, aps = {}, {}
    for name in _NAMES:
        a = np.ascontiguousarray(inputs[name])
        arrays["in_" + name] = a
        aps[name] = nc.dram_tensor("in_" + name, a.shape, mybir.dt.from_np(a.dtype), kind="ExternalInput").ap()
    out = nc.dram_tensor("out_0", inputs["x"].shape, F32, kind="ExternalOutput").ap()
    build(nc, aps, out)
    r = run_bass_kernel_spmd(nc, [arrays], core_ids=[0])
    return r.results[0]["out_0"]
```
